# Optimizing a Trainium2 kernel written in Bass

```python
import numpy as np
import jax
import jax.numpy as jnp

def _softmax(x, axis=-1):
    return jax.nn.softmax(x, axis=axis)

def _gelu(x):
    return jax.nn.gelu(x, approximate=True)

def _silu(x):
    return jax.nn.silu(x)

def _sigmoid(x):
    return jax.nn.sigmoid(x)

def _layernorm(x, axis=-1, eps=1e-05):
    m = jnp.mean(x, axis=axis, keepdims=True)
    v = jnp.var(x, axis=axis, keepdims=True)
    return (x - m) / jnp.sqrt(v + eps)

def _scatter_add(tgt, idx, src, axis=0):
    return tgt.at[idx].add(src)

def _segment_sum(src, seg, n):
    return jax.ops.segment_sum(src, seg, n)
kernel_name = 'mk_recurrent_d1_jaxref_r8_78caa7'

def setup_inputs(seed: int=0):
    np.random.seed(seed)
    _w = jnp.asarray

    def _L0_attn_setup():
        import jax, jax.numpy as jnp
        import numpy as np
        from jax import lax
        H = 64
        P = 64
        N = 128
        G = 8
        K = 4
        D_MODEL = 512
        I = H * P
        GN = G * N
        CONV_DIM = I + 2 * GN
        PROJ = I + CONV_DIM + H
        EPS = 1e-05
        GROUP_SIZE = I // G

        def _reference_tuple_inner(hidden_states, in_proj_w, conv_weight, conv_bias, dt_bias, A_log, D, norm_weight, out_proj_w):
            B, L, _ = hidden_states.shape
            proj = jnp.einsum('bld,pd->blp', hidden_states, in_proj_w)
            gate = proj[..., :I]
            hbc = proj[..., I:I + CONV_DIM]
            dt = proj[..., -H:]
            pad = jnp.pad(hbc, ((0, 0), (K - 1, 0), (0, 0)))
            conv = conv_bias
            for k in range(K):
                conv = conv + pad[:, k:k + L, :] * conv_weight[:, k]
            xBC = jax.nn.silu(conv)
            x = xBC[..., :I].reshape(B, L, H, P)
            Bm = xBC[..., I:I + GN].reshape(B, L, G, N)
            Cm = xBC[..., I + GN:].reshape(B, L, G, N)
            hpg = H // G
            B_h = jnp.repeat(Bm, hpg, axis=2)
            C_h = jnp.repeat(Cm, hpg, axis=2)
            dt_p = jax.nn.softplus(dt + dt_bias)
            A = -jnp.exp(A_log)
            dA = jnp.exp(dt_p * A)
            dtx = dt_p[..., None] * x

            def step(state, inp):
                dA_t, dtx_t, B_t, C_t = inp
                state = state * dA_t[..., None, None] + dtx_t[..., None] * B_t[:, :, None, :]
                y_t = jnp.einsum('bhpn,bhn->bhp', state, C_t)
                return (state, y_t)
            xs = (jnp.moveaxis(dA, 1, 0), jnp.moveaxis(dtx, 1, 0), jnp.moveaxis(B_h, 1, 0), jnp.moveaxis(C_h, 1, 0))
            state0 = jnp.zeros((B, H, P, N), jnp.float32)
            final_state, ys = lax.scan(step, state0, xs)
            y = jnp.moveaxis(ys, 0, 1) + x * D[None, None, :, None]
            y = y.reshape(B, L, I)
            yg = y.reshape(B, L, G, GROUP_SIZE)
            var = jnp.mean(yg * yg, axis=-1, keepdims=True)
            yn = (yg * lax.rsqrt(var + EPS)).reshape(B, L, I) * norm_weight
            yn = yn * jax.nn.silu(gate)
            out = jnp.einsum('bli,di->bld', yn, out_proj_w)
            conv_state_new = jnp.moveaxis(hbc[:, L - (K - 1):, :], 1, 2)
            return (out, conv_state_new, final_state)
        key = jax.random.key(seed)
        ks = jax.random.split(key, 6)
        B, L = (2, 256)
        s = 0.02
        return {'hidden_states': jax.random.normal(ks[0], (B, L, D_MODEL), jnp.float32), 'in_proj_w': jax.random.normal(ks[1], (PROJ, D_MODEL), jnp.float32) * s, 'conv_weight': jax.random.normal(ks[2], (CONV_DIM, K), jnp.float32) * s, 'conv_bias': jnp.zeros((CONV_DIM,), jnp.float32), 'dt_bias': jnp.ones((H,), jnp.float32), 'A_log': jnp.log(jnp.arange(1, H + 1, dtype=jnp.float32)), 'D': jnp.ones((H,), jnp.float32), 'norm_weight': jnp.ones((I,), jnp.float32), 'out_proj_w': jax.random.normal(ks[3], (D_MODEL, I), jnp.float32) * s}
    _L0_attn_in = _L0_attn_setup()

    def _L0_ffn_setup():
        import jax, jax.numpy as jnp
        import numpy as np
        B_, S, D_IN, D_OUT = (4, 256, 512, 512)
        N, RANK, ALPHA = (8, 16, 32)
        SCALE = ALPHA / RANK
        key = jax.random.key(seed)
        kx, ka, kb, kw, kbias = jax.random.split(key, 5)
        x = jax.random.normal(kx, (B_, S, D_IN), dtype=jnp.float32)
        lora_A = jax.random.normal(ka, (N, RANK, D_IN), dtype=jnp.float32) * (1.0 / np.sqrt(D_IN))
        lora_B = jax.random.normal(kb, (N, D_OUT, RANK), dtype=jnp.float32) * (1.0 / np.sqrt(RANK))
        W = jax.random.normal(kw, (D_OUT, D_IN), dtype=jnp.float32) * (1.0 / np.sqrt(D_IN))
        bias = jax.random.normal(kbias, (D_OUT,), dtype=jnp.float32) * 0.01
        lora_weights = jnp.full((N,), 1.0 / N, dtype=jnp.float32)
        return {'x': x, 'lora_A': lora_A, 'lora_B': lora_B, 'W': W, 'bias': bias, 'lora_weights': lora_weights}
    _L0_ffn_in = _L0_ffn_setup()
    _d = {'L0_attn_hidden_states': _L0_attn_in['hidden_states'], 'L0_attn_in_proj_w': _L0_attn_in['in_proj_w'], 'L0_attn_conv_weight': _L0_attn_in['conv_weight'], 'L0_attn_conv_bias': _L0_attn_in['conv_bias'], 'L0_attn_dt_bias': _L0_attn_in['dt_bias'], 'L0_attn_A_log': _L0_attn_in['A_log'], 'L0_attn_D': _L0_attn_in['D'], 'L0_attn_norm_weight': _L0_attn_in['norm_weight'], 'L0_attn_out_proj_w': _L0_attn_in['out_proj_w'], 'L0_ffn_lora_A': _L0_ffn_in['lora_A'], 'L0_ffn_lora_B': _L0_ffn_in['lora_B'], 'L0_ffn_W': _L0_ffn_in['W'], 'L0_ffn_bias': _L0_ffn_in['bias'], 'L0_ffn_lora_weights': _L0_ffn_in['lora_weights']}
    _x0 = _d['L0_attn_hidden_states']
    _d['L0_attn_hidden_states'] = jax.random.normal(jax.random.fold_in(jax.random.key(seed), 1), (2, 1024, 512), dtype=_x0.dtype)
    del _x0
    return _d

def reference(L0_attn_hidden_states, L0_attn_in_proj_w, L0_attn_conv_weight, L0_attn_conv_bias, L0_attn_dt_bias, L0_attn_A_log, L0_attn_D, L0_attn_norm_weight, L0_attn_out_proj_w, L0_ffn_lora_A, L0_ffn_lora_B, L0_ffn_W, L0_ffn_bias, L0_ffn_lora_weights):

    def _L0_attn_ref(hidden_states, in_proj_w, conv_weight, conv_bias, dt_bias, A_log, D, norm_weight, out_proj_w):
        import jax, jax.numpy as jnp
        import numpy as np
        from jax import lax
        H = 64
        P = 64
        N = 128
        G = 8
        K = 4
        D_MODEL = 512
        I = H * P
        GN = G * N
        CONV_DIM = I + 2 * GN
        PROJ = I + CONV_DIM + H
        EPS = 1e-05
        GROUP_SIZE = I // G

        def _reference_tuple_inner(hidden_states, in_proj_w, conv_weight, conv_bias, dt_bias, A_log, D, norm_weight, out_proj_w):
            B, L, _ = hidden_states.shape
            proj = jnp.einsum('bld,pd->blp', hidden_states, in_proj_w)
            gate = proj[..., :I]
            hbc = proj[..., I:I + CONV_DIM]
            dt = proj[..., -H:]
            pad = jnp.pad(hbc, ((0, 0), (K - 1, 0), (0, 0)))
            conv = conv_bias
            for k in range(K):
                conv = conv + pad[:, k:k + L, :] * conv_weight[:, k]
            xBC = jax.nn.silu(conv)
            x = xBC[..., :I].reshape(B, L, H, P)
            Bm = xBC[..., I:I + GN].reshape(B, L, G, N)
            Cm = xBC[..., I + GN:].reshape(B, L, G, N)
            hpg = H // G
            B_h = jnp.repeat(Bm, hpg, axis=2)
            C_h = jnp.repeat(Cm, hpg, axis=2)
            dt_p = jax.nn.softplus(dt + dt_bias)
            A = -jnp.exp(A_log)
            dA = jnp.exp(dt_p * A)
            dtx = dt_p[..., None] * x

            def step(state, inp):
                dA_t, dtx_t, B_t, C_t = inp
                state = state * dA_t[..., None, None] + dtx_t[..., None] * B_t[:, :, None, :]
                y_t = jnp.einsum('bhpn,bhn->bhp', state, C_t)
                return (state, y_t)
            xs = (jnp.moveaxis(dA, 1, 0), jnp.moveaxis(dtx, 1, 0), jnp.moveaxis(B_h, 1, 0), jnp.moveaxis(C_h, 1, 0))
            state0 = jnp.zeros((B, H, P, N), jnp.float32)
            final_state, ys = lax.scan(step, state0, xs)
            y = jnp.moveaxis(ys, 0, 1) + x * D[None, None, :, None]
            y = y.reshape(B, L, I)
            yg = y.reshape(B, L, G, GROUP_SIZE)
            var = jnp.mean(yg * yg, axis=-1, keepdims=True)
            yn = (yg * lax.rsqrt(var + EPS)).reshape(B, L, I) * norm_weight
            yn = yn * jax.nn.silu(gate)
            out = jnp.einsum('bli,di->bld', yn, out_proj_w)
            conv_state_new = jnp.moveaxis(hbc[:, L - (K - 1):, :], 1, 2)
            return (out, conv_state_new, final_state)
        return _reference_tuple_inner(hidden_states, in_proj_w, conv_weight, conv_bias, dt_bias, A_log, D, norm_weight, out_proj_w)[0]

    def _L0_ffn_ref(x, lora_A, lora_B, W, bias, lora_weights):
        import jax, jax.numpy as jnp
        import numpy as np
        B_, S, D_IN, D_OUT = (4, 256, 512, 512)
        N, RANK, ALPHA = (8, 16, 32)
        SCALE = ALPHA / RANK
        h = jnp.einsum('bsd,nrd->nbsr', x, lora_A)
        coef = (SCALE * lora_weights)[:, None, None]
        lora_out = jnp.einsum('nbsr,nor->bso', h, lora_B * coef)
        base = jnp.einsum('bsd,od->bso', x, W) + bias
        return base + lora_out
    x = L0_attn_hidden_states
    xn = _layernorm(x, axis=-1)
    s = _L0_attn_ref(xn, L0_attn_in_proj_w, L0_attn_conv_weight, L0_attn_conv_bias, L0_attn_dt_bias, L0_attn_A_log, L0_attn_D, L0_attn_norm_weight, L0_attn_out_proj_w)
    g = _silu(_L0_ffn_ref(xn, L0_ffn_lora_A, L0_ffn_lora_B, L0_ffn_W, L0_ffn_bias, L0_ffn_lora_weights))
    x = x + s * g
    return x

_drawn_inputs = setup_inputs


def setup_inputs(seed=0):
    import zlib

    import numpy as np

    out = dict(_drawn_inputs(seed))
    spreads = {'L0_attn_conv_bias': (0.0, 0.1),
     'L0_attn_dt_bias': (1.0, 0.6),
     'L0_attn_D': (1.0, 0.2),
     'L0_attn_norm_weight': (1.0, 0.2),
     'L0_ffn_lora_weights': (0.125, 0.2)}
    factors = {'L0_attn_A_log': 64.0, 'L0_ffn_bias': 24.674}
    for name, (base, spread) in spreads.items():
        noise = np.random.default_rng([zlib.crc32(name.encode()), seed]).standard_normal(out[name].shape)
        drawn = base * np.exp(spread * noise) if base else spread * noise
        out[name] = jnp.asarray(drawn.astype(out[name].dtype))
    for name, factor in factors.items():
        out[name] = (out[name] * factor).astype(out[name].dtype)
    return out
```

```python
from contextlib import ExitStack

import concourse.bass as bass
from concourse import mybir

F32 = mybir.dt.float32
F32R = mybir.dt.float32r
ALU = mybir.AluOpType
ACT = mybir.ActivationFunctionType

P = 128
BATCH, SEQ, DM = 2, 1024, 512
HEADS, HD, NS, GROUPS, TAPS = 64, 64, 128, 8, 4
INNER = HEADS * HD
GC = INNER // GROUPS
GH = HEADS // GROUPS
CONV = INNER + 2 * GROUPS * NS
PROJ = INNER + CONV + HEADS
KT = DM // P
XT = GC // P
MT = XT + 2
BLK = 512
NCH = SEQ // P
CPB = BLK // P
NBLK = SEQ // BLK
LORA_N, LORA_R = 8, 16
LORA_SCALE = 32 / 16
EPS = 1e-5
A_LOG_MAX = 88.7
EXP_ZERO = -200.0


class Mark:

    def __init__(self, sem):
        self.sem, self.n = sem, 0


class Slot:

    def __init__(self, buf, mark=None):
        self.buf, self.mark, self.free = buf, mark, []


class Ring:
    def __init__(self, slots):
        self.slots, self.at = slots, -1

    def take(self):
        self.at = (self.at + 1) % len(self.slots)
        return self.slots[self.at]


class Queues:

    def __init__(self):
        self.steps = {k: [] for k in ("tensor", "vector", "scalar", "gpsimd", "sync")}
        self.seen = {k: {} for k in self.steps}

    def do(self, engine, step, after=(), mark=None, by=1):
        for m, n in after:
            if self.seen[engine].get(m, 0) < n:
                self.seen[engine][m] = n
                self.steps[engine].append(lambda e, m=m, n=n: e.wait_ge(m.sem, n))
        if mark is None:
            self.steps[engine].append(step)
            return None
        mark.n += by
        self.steps[engine].append(lambda e: step(e).then_inc(mark.sem, by))
        return mark, mark.n

    def wait(self, engine, after):
        self.do(engine, lambda e: None, after)

    def play(self, engine, e):
        for step in self.steps[engine]:
            step(e)


def build(nc, hidden, w_in_t, conv_w, conv_b, dt_bias, a_log, d_skip, norm_w, w_out_t,
          lora_a, lora_b_t, w_ffn_t, ffn_bias, lora_w, out):
    ctx = ExitStack()
    with ctx:
        def sb(name, shape, dt=F32):
            return ctx.enter_context(nc.sbuf_tensor(name, shape, dt))

        def mark(name):
            return Mark(ctx.enter_context(nc.semaphore(name)))

        def dma_slots(name, shape, n):
            return [Slot(sb(f"{name}{i}", shape), mark(f"landed_{name}{i}")) for i in range(n)]

        q = Queues()
        do = q.do

        decays_d = nc.dram_tensor("decays_d", [BATCH, NCH, HEADS, P], F32).ap()
        totals_d = nc.dram_tensor("totals_d", [BATCH, NCH, HEADS], F32).ap()
        ffn_d = nc.dram_tensor("ffn_d", [BATCH, NCH, P, DM], F32).ap()

        xn_hi = sb("xn_hi", [P, KT, SEQ], F32R)
        xn_lo = sb("xn_lo", [P, KT, SEQ], F32R)
        out_sum = sb("out_sum", [P, NCH, DM])
        wconv_hi = sb("wconv_hi", [P, KT, MT * P], F32R)
        wconv_lo = sb("wconv_lo", [P, KT, MT * P], F32R)
        wgate_hi = sb("wgate_hi", [P, KT, GC], F32R)
        wgate_lo = sb("wgate_lo", [P, KT, GC], F32R)
        wout_hi = sb("wout_hi", [P, XT, DM], F32R)
        wout_lo = sb("wout_lo", [P, XT, DM], F32R)
        stage = dma_slots("stage", [P, KT * GC], 1)[0]
        xc = Ring([Slot(sb(f"xc{i}", [P, MT, BLK])) for i in range(2)])
        halo = Ring([Slot(sb(f"halo{i}", [P, TAPS - 1 + BLK])) for i in range(2)])
        tails = sb("tails", [P, MT, TAPS - 1])
        decay_bc = Ring(dma_slots("decay_bc", [P, GH * P], 2))
        L = Slot(sb("L", [P, GH * P]))
        M = Ring([Slot(sb(f"M{i}", [P, GH * P])) for i in range(2)])
        x_tok = Slot(sb("x_tok", [P, GC]))
        dtx = Ring([Slot(sb(f"dtx{i}", [P, GC])) for i in range(2)])
        skip = Ring([Slot(sb(f"skip{i}", [P, GC])) for i in range(2)])
        xw = Ring([Slot(sb(f"xw{i}", [P, GC])) for i in range(2)])
        b_tok = Ring([Slot(sb(f"b_tok{i}", [P, NS])) for i in range(2)])
        y = Slot(sb("y", [P, GC]))
        sgate = Slot(sb("sgate", [P, GC]))
        yn = Slot(sb("yn", [P, GC]))
        ynt_hi = Slot(sb("ynt_hi", [P, XT, P], F32R))
        ynt_lo = Slot(sb("ynt_lo", [P, XT, P], F32R))
        state = Ring([Slot(sb(f"state{i}", [NS, GC])) for i in range(2)])
        state_dec = Slot(sb("state_dec", [NS, GC]))
        prefix_dt = Slot(sb("prefix_dt", [P, NCH, P]))
        total_bc = Slot(sb("total_bc", [P, NCH * HEADS]), mark("landed_total"))
        io = Ring(dma_slots("io", [P, DM], 2))
        eye8 = sb("eye8", [P, GH, P])
        convw_sb = sb("convw_sb", [P, CONV // P, TAPS])
        convb_sb = sb("convb_sb", [P, CONV // P])
        normw_sb = sb("normw_sb", [P, INNER // P])
        skip_bc = sb("skip_bc", [P, HEADS])
        dtb_sb = sb("dtb_sb", [P, 1])
        nega_sb = sb("nega_sb", [P, 1])
        loraw_sb = sb("loraw_sb", [P, 1])
        half = sb("half", [P, 1])
        stats = sb("stats", [P, 6])
        mean_var = sb("mean_var", [P, 2])
        rs = sb("rs", [P, 4])
        eye = eye8[:, 0, :]

        def bank(name):
            return ctx.enter_context(nc.psum_tensor(name, [P, 512], F32))

        big = Ring([Slot(bank(f"big{i}")) for i in range(2)])
        turned = Ring([Slot(bank(f"turned{i}")) for i in range(2)])
        ps_g = Slot(bank("ps_g"))
        ps_u = Slot(bank("ps_u"))
        ps_in = Slot(bank("ps_in"))
        ps_cs = Slot(bank("ps_cs"))

        names = """par eye half nega loraw stat mv var rstd norm turn_x hi lo loraB wffn mm_ffn
            ffn_wh ffn_wl biased ffn_act ffn_st mm_dt z absz e u negc lnu ru cru dt da dstart dz
            pfx st_dec st_tot mm_pt pt mm_conv h_full h_head h_tail tap0 taps silu
            w_hi w_lo mm_t mm_bt mm_g xt bt dtx skip scan M xw mm_cs mm_in mm_u mm_gate cs
            y1 y2 sdec state ssq var2 rstd2 sgate yn mm_ynt hi2 lo2 mm_out osum fin1 fin2 fin3
            stored""".split()
        k = {n: mark("s_" + n) for n in names}

        def three_passes(psum, pairs, after, done):
            n = len(pairs) * 3
            i = 0
            for a_hi, a_lo, b_hi, b_lo in pairs:
                for a, b in ((a_hi, b_hi), (a_hi, b_lo), (a_lo, b_hi)):
                    i += 1
                    tok = do("tensor", lambda e, a=a, b=b, i=i: e.matmul(
                        psum, a, b, start=(i == 1), stop=(i == n)),
                        after if i == 1 else (), done if i == n else None)
            return tok

        small = [(convw_sb[:, :, :], conv_w),
                 (convb_sb[:, :], conv_b),
                 (normw_sb[:, :], norm_w),
                 (skip_bc[:, :], d_skip.partition_broadcast(P)),
                 (dtb_sb[0:HEADS, :], dt_bias), (dtb_sb[HEADS:P, :], dt_bias),
                 (nega_sb[0:HEADS, :], a_log), (nega_sb[HEADS:P, :], a_log),
                 (loraw_sb[:, :], lora_w)]
        for dst, src in small:
            params = do("scalar", lambda e, dst=dst, src=src: e.dma_start(dst, src), (), k["par"], 16)
        zeroed = do("gpsimd", lambda e: e.memset(eye8[:, :, :], 0.0), (), k["eye"])
        eye_ready = do("gpsimd", lambda e: e.affine_select(
            out=eye8[:, :, :], in_=eye8[:, :, :], compare_op=ALU.not_equal, fill=1.0, base=0,
            pattern=[[0, GH], [-1, P]], channel_multiplier=1), [zeroed], k["eye"])
        half_ready = do("gpsimd", lambda e: e.memset(half[:, :], -0.5), (), k["half"])
        t = do("vector", lambda e: e.tensor_scalar(nega_sb[:, :], nega_sb[:, :], A_LOG_MAX, None, ALU.min),
               [params], k["nega"])
        t = do("scalar", lambda e: e.activation(nega_sb[:, :], nega_sb[:, :], ACT.Exp), [t], k["nega"])
        nega_ready = do("vector", lambda e: e.tensor_scalar(nega_sb[:, :], nega_sb[:, :], -1.0, None, ALU.mult),
                        [t], k["nega"])
        loraw_ready = do("vector", lambda e: e.tensor_scalar(loraw_sb[:, :], loraw_sb[:, :], LORA_SCALE, None,
                                                             ALU.mult), [params], k["loraw"])

        w_free = {"conv": [], "gate": [], "out": []}
        w_ready = {}

        def load_weight(dst_key, src, hi, lo, cols, scale=None):
            raw = stage.buf[:, 0:KT * cols].rearrange("p (t c) -> p t c", t=KT)
            landed = do("sync", lambda e: e.dma_start(raw, src), stage.free, stage.mark, 16)
            free = w_free[dst_key]
            if scale is None:
                h = do("scalar", lambda e: e.activation(hi, raw, ACT.Copy), [landed] + free, k["w_hi"])
                l = do("gpsimd", lambda e: e.tensor_tensor(lo, raw, hi.bitcast(F32), ALU.subtract),
                       [landed, h] + free, k["w_lo"])
            else:
                for t in range(KT):
                    h = do("scalar", lambda e, t=t: e.activation(
                        hi[:, t, :], raw[:, t, :], ACT.Copy, scale=scale[:, t:t + 1]),
                        [landed, params] + free, k["w_hi"])
                for t in range(KT):
                    l = do("vector", lambda e, t=t: e.scalar_tensor_tensor(
                        lo[:, t, :], raw[:, t, :], scale[:, t:t + 1], hi[:, t, :].bitcast(F32),
                        ALU.mult, ALU.subtract), [landed, h, params] + free, k["w_lo"])
            stage.free = [h, l]
            return [h, l]

        def in_cols(a, n):
            return w_in_t[:, a:a + n].rearrange("(t p) c -> p t c", p=P)

        def load_conv_x(g):
            w_ready["conv_x"] = load_weight("conv", in_cols(INNER + g * GC, GC),
                                            wconv_hi[:, :, 0:GC], wconv_lo[:, :, 0:GC], GC)

        def load_conv_bc(g):
            raw = stage.buf[:, 0:KT * 2 * NS].rearrange("p (t c) -> p t c", t=KT)
            landed = []
            for i in range(2):
                landed.append(do("sync", lambda e, i=i: e.dma_start(
                    raw[:, :, i * NS:(i + 1) * NS], in_cols(2 * INNER + (i * GROUPS + g) * NS, NS)),
                    stage.free, stage.mark, 16))
            hi, lo = wconv_hi[:, :, GC:MT * P], wconv_lo[:, :, GC:MT * P]
            h = do("scalar", lambda e: e.activation(hi, raw, ACT.Copy), landed + w_free["conv"], k["w_hi"])
            l = do("gpsimd", lambda e: e.tensor_tensor(lo, raw, hi.bitcast(F32), ALU.subtract),
                   landed + [h] + w_free["conv"], k["w_lo"])
            stage.free = [h, l]
            w_ready["conv_bc"] = [h, l]

        def load_gate(g):
            w_ready["gate"] = load_weight("gate", in_cols(g * GC, GC), wgate_hi[:, :, :],
                                          wgate_lo[:, :, :], GC)

        def load_out(g):
            w_ready["out"] = load_weight(
                "out", w_out_t[g * GC:(g + 1) * GC, :].rearrange("(t p) c -> p t c", p=P),
                wout_hi[:, :, :], wout_lo[:, :, :], DM, normw_sb[:, g * XT:(g + 1) * XT])

        xn_free = []
        xn_ready = []

        def layer_norm(b):
            nonlocal xn_ready
            for c in range(NCH):
                tile = io.take()
                landed = do("sync", lambda e, tile=tile, c=c: e.dma_start(
                    tile.buf[:, :], hidden[b, c * P:(c + 1) * P, :]), tile.free, tile.mark, 16)
                before = [(k["norm"], k["norm"].n)]
                s = do("vector", lambda e, tile=tile: e.bn_stats(stats[:, :], tile.buf[:, :]),
                       [landed] + before, k["stat"])
                s = do("vector", lambda e: e.bn_aggr(mean_var[:, :], stats[:, :]), [s], k["mv"])
                s = do("gpsimd", lambda e: e.tensor_scalar(rs[:, 0:1], mean_var[:, 1:2], EPS, None, ALU.add),
                       [s] + before, k["var"])
                r = do("gpsimd", lambda e: e.tensor_tensor(rs[:, 1:2], rs[:, 0:1], half[:, :], ALU.pow),
                       [s, half_ready], k["rstd"])
                nrm = do("vector", lambda e, tile=tile: e.tensor_scalar(
                    tile.buf[:, :], tile.buf[:, :], mean_var[:, 0:1], rs[:, 1:2], ALU.subtract, ALU.mult),
                    [r], k["norm"])
                ps = turned.take()
                for t in range(KT):
                    tr = do("tensor", lambda e, t=t, ps=ps, tile=tile: e.transpose(
                        ps.buf[:, t * P:(t + 1) * P], tile.buf[:, t * P:(t + 1) * P], eye),
                        [nrm, eye_ready] + ps.free, k["turn_x"] if t == KT - 1 else None)
                tile.free = [tr]
                src = ps.buf[:, :].rearrange("p (t c) -> p t c", t=KT)
                cols = slice(c * P, (c + 1) * P)
                h = do("scalar", lambda e, src=src, cols=cols: e.activation(
                    xn_hi[:, :, cols], src, ACT.Copy), [tr] + xn_free, k["hi"])
                l = do("vector", lambda e, src=src, cols=cols: e.tensor_tensor(
                    xn_lo[:, :, cols], src, xn_hi[:, :, cols].bitcast(F32), ALU.subtract),
                    [h] + xn_free, k["lo"])
                ps.free = [l]
            xn_ready = [h, l]

        def step_sizes(b):
            raw = stage.buf[:, 0:KT * P].rearrange("p (t c) -> p t c", t=KT)
            landed = [do("sync", lambda e, i=i: e.dma_start(
                raw[:, :, i * HEADS:(i + 1) * HEADS], in_cols(INNER + CONV, HEADS)),
                stage.free, stage.mark, 16) for i in range(2)]
            hi, lo = wgate_hi[:, :, 0:P], wgate_lo[:, :, 0:P]
            h = do("scalar", lambda e: e.activation(hi, raw, ACT.Copy), landed + w_free["gate"], k["w_hi"])
            l = do("gpsimd", lambda e: e.tensor_tensor(lo, raw, hi.bitcast(F32), ALU.subtract),
                   landed + [h] + w_free["gate"], k["w_lo"])
            stage.free = [h, l]
            zs, es, us, ds = (s.buf for s in (L, M.slots[0], M.slots[1], decay_bc.slots[0]))
            free = L.free + M.slots[0].free + M.slots[1].free + decay_bc.slots[0].free
            for j in range(NBLK):
                cols = slice(j * BLK, (j + 1) * BLK)
                ps = big.take()
                mm = three_passes(ps.buf[:, :], [(hi[:, t, :], lo[:, t, :], xn_hi[:, t, cols],
                                                  xn_lo[:, t, cols]) for t in range(KT)],
                                  [h, l] + xn_ready + ps.free, k["mm_dt"])
                z = do("scalar", lambda e, ps=ps, cols=cols: e.activation(
                    zs[:, cols], ps.buf[:, :], ACT.Identity, bias=dtb_sb[:, 0:1]), [mm, params] + free, k["z"])
                ps.free = [z]
            w_free["gate"] = [mm]
            t = do("vector", lambda e: e.scalar_tensor_tensor(es[:, :], zs[:, :], -1.0, zs[:, :],
                                                              ALU.mult, ALU.min), [z] + free, k["absz"])
            t = do("scalar", lambda e: e.activation(es[:, :], es[:, :], ACT.Exp), [t], k["e"])
            u = do("vector", lambda e: e.tensor_scalar(us[:, :], es[:, :], 1.0, None, ALU.add), [t] + free, k["u"])
            nc_ = do("vector", lambda e: e.scalar_tensor_tensor(es[:, :], us[:, :], -1.0, es[:, :],
                                                                ALU.add, ALU.subtract), [u], k["negc"])
            ln = do("scalar", lambda e: e.activation(ds[:, :], us[:, :], ACT.Ln), [u] + free, k["lnu"])
            ru = do("vector", lambda e: e.reciprocal(us[:, :], us[:, :]), [ln, nc_], k["ru"])
            t = do("vector", lambda e: e.tensor_tensor(es[:, :], es[:, :], us[:, :], ALU.mult), [ru], k["cru"])
            t = do("vector", lambda e: e.tensor_tensor(ds[:, :], ds[:, :], es[:, :], ALU.subtract), [t, ln], k["dt"])
            dt = do("vector", lambda e: e.scalar_tensor_tensor(ds[:, :], zs[:, :], 0.0, ds[:, :],
                                                               ALU.max, ALU.add), [t], k["dt"])
            t = do("vector", lambda e: e.tensor_scalar(us[:, :], ds[:, :], nega_sb[:, 0:1], EXP_ZERO,
                                                       ALU.mult, ALU.max), [dt, nega_ready], k["da"])
            da = do("scalar", lambda e: e.activation(us[:, :], us[:, :], ACT.Exp), [t], k["da"])
            heads = slice(0, HEADS)
            starts = lambda buf: buf[:, :].rearrange("p (c i) -> p c i", i=P)[heads, :, 0:1]
            t0 = do("vector", lambda e: e.tensor_copy(es[:, :], us[:, :]), [da], k["dz"])
            t1 = do("vector", lambda e: e.memset(zs[:, :], 0.0), [dt], k["dstart"])
            dz = do("vector", lambda e: e.memset(starts(es), 0.0), [t0], k["dz"])
            d1 = do("vector", lambda e: e.tensor_copy(starts(zs), starts(us)), [t1, da], k["dstart"])
            pfx = do("vector", lambda e: e.tensor_tensor_scan(ds[heads, :], es[heads, :], zs[heads, :], 0.0,
                                                              ALU.mult, ALU.add), [dz, d1, da], k["pfx"])
            std = do("sync", lambda e: e.dma_start(
                decays_d[b].rearrange("c h i -> h c i"),
                es[heads, :].rearrange("h (c i) -> h c i", i=P)), [dz], k["st_dec"], 16)
            for j in range(2):
                ps = turned.take()
                for i in range(4):
                    mm = do("tensor", lambda e, i=i, j=j, ps=ps: e.transpose(
                        ps.buf[:, i * P:(i + 1) * P], ds[:, (4 * j + i) * P:(4 * j + i + 1) * P], eye),
                        [pfx] + ps.free, k["mm_pt"] if i == 3 else None)
                cp = do("scalar", lambda e, j=j, ps=ps: e.activation(
                    prefix_dt.buf[:, 4 * j:4 * j + 4, :], ps.buf[:, :].rearrange("p (c i) -> p c i", i=P),
                    ACT.Copy), [mm] + prefix_dt.free, k["pt"])
                ps.free = [cp]
            stt = do("sync", lambda e: e.dma_start(totals_d[b:b + 1], prefix_dt.buf[P - 1:P, :, 0:HEADS]),
                     [cp], k["st_tot"], 16)
            do("sync", lambda e: e.dma_start(
                total_bc.buf[:, :], totals_d[b].rearrange("c h -> (c h)").partition_broadcast(P)),
                [stt] + total_bc.free, total_bc.mark, 16)
            L.free = [pfx]
            M.slots[0].free = [pfx, std]
            M.slots[1].free = [d1, da]
            decay_bc.slots[0].free = [mm]
            return cp, std

        def ffn(b):
            nonlocal_free = xc.slots[1].free
            scratch = xc.slots[1].buf[:, :, :].rearrange("p m c -> p (m c)")
            la, lb, lbs, bias = (scratch[:, i * DM:(i + 1) * DM] for i in range(4))
            par = k["wffn"]
            for dst, src in ((la, lora_a), (lb, lora_b_t), (bias, ffn_bias.partition_broadcast(P))):
                got = do("sync", lambda e, dst=dst, src=src: e.dma_start(dst, src), nonlocal_free, par, 16)
            raw = stage.buf[:, :].rearrange("p (t c) -> p t c", t=KT)
            landed = do("sync", lambda e: e.dma_start(raw, w_ffn_t.rearrange("(t p) c -> p t c", p=P)),
                        stage.free, stage.mark, 16)
            lbr = do("vector", lambda e: e.tensor_scalar(lbs, lb, loraw_sb[:, 0:1], None, ALU.mult),
                     [got, loraw_ready] + nonlocal_free, k["loraB"])
            for t in range(KT):
                ps = big.take()
                mm = do("tensor", lambda e, t=t, ps=ps: e.matmul(
                    ps.buf[:, :], la[:, t * P:(t + 1) * P], lbs, start=True, stop=True),
                    [lbr, got] + ps.free, k["mm_ffn"])
                w = do("vector", lambda e, t=t, ps=ps: e.tensor_tensor(
                    raw[:, t, :], raw[:, t, :], ps.buf[:, :], ALU.add), [mm, landed], k["ffn_wl"])
                ps.free = [w]
                h = do("scalar", lambda e, t=t: e.activation(wgate_hi[:, t, :], raw[:, t, :], ACT.Copy),
                       [w] + w_free["gate"], k["w_hi"])
                l = do("vector", lambda e, t=t: e.tensor_tensor(
                    wgate_lo[:, t, :], raw[:, t, :], wgate_hi[:, t, :].bitcast(F32), ALU.subtract),
                    [h] + w_free["gate"], k["ffn_wl"])
            stage.free = [h, l]
            outs = Ring([sgate, x_tok])
            for c in range(NCH):
                cols = slice(c * P, (c + 1) * P)
                ps = big.take()
                mm = three_passes(ps.buf[:, :], [(xn_hi[:, t, cols], xn_lo[:, t, cols], wgate_hi[:, t, :],
                                                  wgate_lo[:, t, :]) for t in range(KT)],
                                  [h, l] + xn_ready + ps.free, k["mm_ffn"])
                bd = do("vector", lambda e, ps=ps: e.tensor_tensor(y.buf[:, :], ps.buf[:, :], bias, ALU.add),
                        [mm, got] + y.free, k["biased"])
                ps.free = [bd]
                o = outs.take()
                a = do("scalar", lambda e, o=o: e.activation(o.buf[:, :], y.buf[:, :], ACT.Silu),
                       [bd] + o.free, k["ffn_act"])
                y.free = [a]
                st = do("sync", lambda e, o=o, c=c: e.dma_start(ffn_d[b, c], o.buf[:, :]), [a],
                        ffn_stored[c % 2], 16)
                o.free = [st]
            w_free["gate"] = [mm]
            xc.slots[1].free = [bd]

        ffn_stored = [mark("ffn_stored0"), mark("ffn_stored1")]

        tail_ready = [None] * MT
        pending_silu = []

        def flush_silu():
            for f in pending_silu:
                f()
            pending_silu.clear()

        def conv_tile(g, blk, m, slot, ready):
            tile = g * XT + m if m < XT else INNER // P + (m - XT) * GROUPS + g
            cols = slice(blk * BLK, (blk + 1) * BLK)
            mc = slice(m * P, (m + 1) * P)
            ps = big.take()
            mm = three_passes(ps.buf[:, :], [(wconv_hi[:, t, mc], wconv_lo[:, t, mc], xn_hi[:, t, cols],
                                              xn_lo[:, t, cols]) for t in range(KT)],
                              w_ready["conv_x" if m < XT else "conv_bc"] + xn_ready + ps.free, k["mm_conv"])
            h = halo.take()
            hb, acc = h.buf, slot.buf[:, m, :]
            full = do("scalar", lambda e: e.activation(hb[:, TAPS - 1:], ps.buf[:, :], ACT.Copy),
                      [mm] + h.free, k["h_full"])
            t0 = do("scalar", lambda e: e.activation(
                acc, ps.buf[:, :], ACT.Identity, bias=convb_sb[:, tile:tile + 1],
                scale=convw_sb[:, tile, TAPS - 1:TAPS]), [params] + slot.free, k["tap0"])
            ps.free = [t0, full]
            if blk == 0:
                head = do("gpsimd", lambda e: e.memset(hb[:, 0:TAPS - 1], 0.0), h.free, k["h_head"])
            else:
                head = do("gpsimd", lambda e: e.tensor_copy(hb[:, 0:TAPS - 1], tails[:, m, :]),
                          h.free + [tail_ready[m]], k["h_head"])
            h.free = []
            if blk < NBLK - 1:
                tail_ready[m] = do("gpsimd", lambda e: e.tensor_copy(tails[:, m, :], hb[:, BLK:]),
                                   [full, head], k["h_tail"])
                h.free = [tail_ready[m]]
            tok = t0
            for i in range(TAPS - 1):
                tok = do("vector", lambda e, i=i: e.scalar_tensor_tensor(
                    acc, hb[:, i:i + BLK], convw_sb[:, tile, i:i + 1], acc, ALU.mult, ALU.add),
                    [tok, full, head], k["taps"])
            h.free = h.free + [tok]

            def silu(tok=tok):
                s = do("scalar", lambda e: e.activation(acc, acc, ACT.Silu), [tok], k["silu"])
                ready[m] = s
            flush_silu()
            pending_silu.append(silu)
            return mm

        def heads_bc(ap, n=HD):
            return ap.unsqueeze(2).to_broadcast([P, GH, n])

        def by_head(ap):
            return ap.rearrange("p (h c) -> p h c", h=GH)

        def fetch_decays(ch):
            b, g, c = ch["b"], ch["g"], ch["c"]
            d = ch["decay"] = decay_bc.take()
            src = decays_d[b, c, g * GH:(g + 1) * GH, :].rearrange("h i -> (h i)").partition_broadcast(P)
            ch["landed"] = do("sync", lambda e: e.dma_start(d.buf[:, :], src),
                              d.free + [ch["decays_stored"]], d.mark, 16)

        def load_stage(ch):
            g, c, slot, ready = ch["g"], ch["c"], ch["slot"], ch["ready"]
            cc = slice((c % CPB) * P, (c % CPB + 1) * P)
            ps = turned.take()
            for m in range(XT):
                tr = do("tensor", lambda e, m=m: e.transpose(
                    ps.buf[:, m * P:(m + 1) * P], slot.buf[:, m, cc], eye),
                    [ready[m], eye_ready] + ps.free, k["mm_t"] if m == XT - 1 else None)
            bt = do("tensor", lambda e: e.transpose(ps_u.buf[:, 0:P], slot.buf[:, XT, cc], eye),
                    [ready[XT]] + ps_u.free, k["mm_bt"])
            gm = do("tensor", lambda e: e.matmul(ps_g.buf[:, 0:P], slot.buf[:, XT, cc], slot.buf[:, XT + 1, cc],
                                                 start=True, stop=True),
                    [ready[XT + 1]] + ps_g.free, k["mm_g"])
            xt = do("scalar", lambda e: e.activation(x_tok.buf[:, :], ps.buf[:, :], ACT.Copy),
                    [tr] + x_tok.free, k["xt"])
            ps.free = [xt]
            b_ = ch["b_tok"] = b_tok.take()
            ch["bt"] = do("scalar", lambda e: e.activation(b_.buf[:, :], ps_u.buf[:, 0:P], ACT.Copy),
                          [bt] + b_.free, k["bt"])
            ps_u.free = [ch["bt"]]
            dt_cols = prefix_dt.buf[:, c, HEADS + g * GH:HEADS + (g + 1) * GH]
            dx = ch["dtx"] = dtx.take()
            ch["dtx_t"] = do("vector", lambda e: e.tensor_tensor(
                by_head(dx.buf[:, :]), by_head(x_tok.buf[:, :]), heads_bc(dt_cols), ALU.mult),
                [xt, ch["pt"]] + dx.free, k["dtx"])
            sk = ch["skip"] = skip.take()
            ch["skip_t"] = do("gpsimd", lambda e: e.tensor_tensor(
                by_head(sk.buf[:, :]), by_head(x_tok.buf[:, :]),
                heads_bc(skip_bc[:, g * GH:(g + 1) * GH]), ALU.mult), [xt, params] + sk.free, k["skip"])
            x_tok.free = [ch["dtx_t"], ch["skip_t"]]
            d = ch["decay"]
            sc = do("vector", lambda e: e.tensor_tensor_scan(
                L.buf[:, :], d.buf[:, :], eye8[:, :, :].rearrange("p h i -> p (h i)"), 0.0,
                ALU.mult, ALU.add), [ch["landed"], eye_ready] + L.free, k["scan"])
            d.free = [sc]
            mx = ch["M"] = M.take()
            ch["M_t"] = do("vector", lambda e: e.tensor_tensor(
                by_head(mx.buf[:, :]), by_head(L.buf[:, :]),
                ps_g.buf[:, 0:P].unsqueeze(1).to_broadcast([P, GH, P]), ALU.mult),
                [sc, gm] + mx.free, k["M"])
            ps_g.free = [ch["M_t"]]
            L.free = [ch["M_t"]]
            if c < NCH - 1:
                w = ch["xw"] = xw.take()
                ch["xw_t"] = do("vector", lambda e: e.tensor_tensor(
                    by_head(w.buf[:, :]), by_head(dx.buf[:, :]),
                    by_head(L.buf[:, :])[:, :, P - 1:P].to_broadcast([P, GH, HD]), ALU.mult),
                    [ch["dtx_t"], sc] + w.free, k["xw"])
                L.free = [ch["M_t"], ch["xw_t"]]

        def gate_stage(ch):
            c = ch["c"]
            cols = slice(c * P, (c + 1) * P)
            ps = big.take()
            mm = three_passes(ps.buf[:, :], [(xn_hi[:, t, cols], xn_lo[:, t, cols], wgate_hi[:, t, :],
                                              wgate_lo[:, t, :]) for t in range(KT)],
                              w_ready["gate"] + xn_ready + ps.free, k["mm_gate"])
            w_free["gate"] = [mm]
            ch["sgate_t"] = do("scalar", lambda e: e.activation(sgate.buf[:, :], ps.buf[:, :], ACT.Silu),
                               [mm] + sgate.free, k["sgate"])
            ps.free = [ch["sgate_t"]]

        def mix_stage(ch):
            g, c, slot = ch["g"], ch["c"], ch["slot"]
            cc = slice((c % CPB) * P, (c % CPB + 1) * P)
            dx, mx = ch["dtx"], ch["M"]
            tok = None
            if c > 0:
                s = ch["state_in"]
                tok = do("tensor", lambda e: e.matmul(ps_cs.buf[:, :], slot.buf[:, XT + 1, cc], s.buf[:, :],
                                                      start=True, stop=True),
                         [ch["state_t"]] + ps_cs.free, k["mm_cs"])
            for h in range(GH):
                n = 2 * HD if h < GH - 1 else HD
                mi = do("tensor", lambda e, h=h, n=n: e.matmul(
                    ps_in.buf[:, h * HD:h * HD + n], mx.buf[:, h * P:(h + 1) * P],
                    dx.buf[:, h * HD:h * HD + n], start=True, stop=True, skip_group_check=True),
                    [ch["M_t"], ch["dtx_t"]] + ps_in.free, k["mm_in"] if h == GH - 1 else None)
            dx.free, mx.free = [mi], [mi]
            if c < NCH - 1:
                w, b_ = ch["xw"], ch["b_tok"]
                mu = do("tensor", lambda e: e.matmul(ps_u.buf[:, :], b_.buf[:, :], w.buf[:, :],
                                                     start=True, stop=True),
                        [ch["xw_t"], ch["bt"]] + ps_u.free, k["mm_u"])
                w.free, b_.free = [mu], [mu]
            ch["last_pe"] = mi
            if c > 0:
                cs = do("vector", lambda e: e.tensor_tensor(
                    by_head(y.buf[:, :]), by_head(ps_cs.buf[:, :]),
                    heads_bc(prefix_dt.buf[:, c, g * GH:(g + 1) * GH]), ALU.mult),
                    [tok, ch["pt"]] + y.free, k["cs"])
                ps_cs.free = [cs]
                y1 = do("vector", lambda e: e.tensor_tensor(y.buf[:, :], ps_in.buf[:, :], y.buf[:, :], ALU.add),
                        [mi, cs], k["y1"])
                ps_in.free = [y1]
            sk = ch["skip"]
            if c < NCH - 1:
                new = state.take()
                if c > 0:
                    st = do("vector", lambda e: e.tensor_tensor(
                        new.buf[:, :], ps_u.buf[:, :], state_dec.buf[:, :], ALU.add),
                        [mu, ch["sdec_t"]] + new.free, k["state"])
                    state_dec.free = [st]
                else:
                    st = do("vector", lambda e: e.tensor_copy(new.buf[:, :], ps_u.buf[:, :]),
                            [mu] + new.free, k["state"])
                ps_u.free = [st]
                ch["next"]["state_in"], ch["next"]["state_t"] = new, st
            if c > 0:
                y2 = do("vector", lambda e: e.tensor_tensor(y.buf[:, :], y.buf[:, :], sk.buf[:, :], ALU.add),
                        [y1, ch["skip_t"]], k["y2"])
            else:
                y2 = do("vector", lambda e: e.tensor_tensor(y.buf[:, :], ps_in.buf[:, :], sk.buf[:, :], ALU.add),
                        [mi, ch["skip_t"]] + y.free, k["y2"])
                ps_in.free = [y2]
            sk.free = [y2]
            ch["y2"] = y2
            if 0 < c + 1 < NCH - 1:
                tot = total_bc.buf[:, (c + 1) * HEADS + g * GH:(c + 1) * HEADS + (g + 1) * GH]
                ch["next"]["sdec_t"] = do("gpsimd", lambda e: e.tensor_tensor(
                    by_head(state_dec.buf[:, :]), by_head(new.buf[:, :]), heads_bc(tot), ALU.mult),
                    [st, (total_bc.mark, total_bc.mark.n)] + state_dec.free, k["sdec"])
                new.free = [ch["next"]["sdec_t"]]
            else:
                if c < NCH - 1:
                    new.free = []
            if c > 0:
                ch["state_in"].free = ch["state_in"].free + [tok]

        def norm_stage(ch):
            sq = do("scalar", lambda e: e.activation(yn.buf[:, :], y.buf[:, :], ACT.Square,
                                                     accum_out=rs[:, 2:3]),
                    [ch["y2"]] + yn.free + [(k["rstd2"], k["rstd2"].n)], k["ssq"])
            v = do("gpsimd", lambda e: e.tensor_scalar(rs[:, 3:4], rs[:, 2:3], 1.0 / GC, EPS, ALU.mult, ALU.add),
                   [sq], k["var2"])
            ch["rstd_t"] = do("gpsimd", lambda e: e.tensor_tensor(rstd_col[:, :], rs[:, 3:4], half[:, :], ALU.pow),
                              [v, half_ready, (k["yn"], k["yn"].n)], k["rstd2"])

        rstd_col = sb("rstd_col", [P, 1])

        def gated_stage(ch):
            ch["yn_t"] = do("vector", lambda e: e.scalar_tensor_tensor(
                yn.buf[:, :], y.buf[:, :], rstd_col[:, 0:1], sgate.buf[:, :], ALU.mult, ALU.mult),
                [ch["rstd_t"], ch["sgate_t"]], k["yn"])
            y.free = [ch["yn_t"]]
            sgate.free = [ch["yn_t"]]

        def turn_stage(ch):
            ps = turned.take()
            for t in range(XT):
                tr = do("tensor", lambda e, t=t: e.transpose(
                    ps.buf[:, t * P:(t + 1) * P], yn.buf[:, t * P:(t + 1) * P], eye),
                    [ch["yn_t"]] + ps.free, k["mm_ynt"] if t == XT - 1 else None)
            yn.free = [tr]
            src = ps.buf[:, :].rearrange("p (t c) -> p t c", t=XT)
            h = do("scalar", lambda e: e.activation(ynt_hi.buf[:, :, :], src, ACT.Copy),
                   [tr] + ynt_hi.free, k["hi2"])
            l = do("vector", lambda e: e.tensor_tensor(ynt_lo.buf[:, :, :], src, ynt_hi.buf[:, :, :].bitcast(F32),
                                                       ALU.subtract), [h] + ynt_lo.free, k["lo2"])
            ps.free = [l]
            ch["ynt"] = [h, l]

        def project_stage(ch):
            b, g, c = ch["b"], ch["g"], ch["c"]
            ps = big.take()
            mm = three_passes(ps.buf[:, :], [(ynt_hi.buf[:, t, :], ynt_lo.buf[:, t, :], wout_hi[:, t, :],
                                              wout_lo[:, t, :]) for t in range(XT)],
                              w_ready["out"] + ch["ynt"] + ps.free, k["mm_out"])
            ynt_hi.free = ynt_lo.free = [mm]
            w_free["out"] = [mm]
            acc = out_sum[:, c, :]
            if g == 0:
                o = do("vector", lambda e: e.tensor_copy(acc, ps.buf[:, :]), [mm] + stored[c], k["osum"])
            else:
                o = do("vector", lambda e: e.tensor_tensor(acc, acc, ps.buf[:, :], ALU.add),
                       [mm, sum_ready[c]], k["osum"])
            ps.free = [o]
            sum_ready[c] = o
            if g == GROUPS - 1:
                xt, ft = io.take(), io.take()
                lx = do("sync", lambda e: e.dma_start(xt.buf[:, :], hidden[b, c * P:(c + 1) * P, :]),
                        xt.free, xt.mark, 16)
                lf = do("sync", lambda e: e.dma_start(ft.buf[:, :], ffn_d[b, c]),
                        ft.free + [(m, m.n) for m in ffn_stored], ft.mark, 16)
                f = do("gpsimd", lambda e: e.tensor_tensor(acc, acc, ft.buf[:, :], ALU.mult), [o, lf], k["fin1"])
                ft.free = [f]
                f = do("gpsimd", lambda e: e.tensor_tensor(acc, acc, xt.buf[:, :], ALU.add), [f, lx], k["fin2"])
                xt.free = [f]
                stored[c] = [do("sync", lambda e: e.dma_start(out[b, c * P:(c + 1) * P, :], acc), [f],
                                k["stored"], 16)]

        stored = [[] for _ in range(NCH)]
        sum_ready = [None] * NCH

        NG = GROUPS * NBLK
        for b in range(BATCH):
            layer_norm(b)
            pt, decays_stored = step_sizes(b)
            ffn(b)
            load_conv_x(0)
            load_conv_bc(0)
            load_gate(0)
            load_out(0)
            blocks = []
            for i in range(NG):
                blocks.append(dict(g=i // NBLK, blk=i % NBLK, slot=xc.slots[i % 2], ready=[None] * MT))
            chunks = []
            for i in range(NG):
                for j in range(CPB):
                    chunks.append(dict(b=b, g=blocks[i]["g"], c=blocks[i]["blk"] * CPB + j, slot=blocks[i]["slot"],
                                       ready=blocks[i]["ready"], pt=pt, decays_stored=decays_stored, block=i))
            for a, nxt in zip(chunks, chunks[1:]):
                a["next"] = nxt
            tiles = [[0, 1], [2, 3], [4], [5]]
            bl = blocks[0]
            for m in range(MT):
                mm = conv_tile(bl["g"], bl["blk"], m, bl["slot"], bl["ready"])
            flush_silu()
            fetch_decays(chunks[0])
            n = len(chunks)
            for i in range(n + 3):
                if i + 1 < n:
                    fetch_decays(chunks[i + 1])
                if i < n:
                    load_stage(chunks[i])
                if i >= 3:
                    project_stage(chunks[i - 3])
                    if chunks[i - 3]["c"] == NCH - 1 and chunks[i - 3]["g"] + 1 < GROUPS:
                        load_out(chunks[i - 3]["g"] + 1)
                if 2 <= i < n + 2:
                    turn_stage(chunks[i - 2])
                if 1 <= i < n + 1:
                    ch = chunks[i - 1]
                    gate_stage(ch)
                    mix_stage(ch)
                    norm_stage(ch)
                    if ch["c"] == NCH - 1 and ch["g"] + 1 < GROUPS:
                        load_gate(ch["g"] + 1)
                    if ch["c"] % CPB == CPB - 1:
                        ch["slot"].free = [ch["last_pe"]]
                if i < n:
                    nb = chunks[i]["block"] + 1
                    if nb < NG:
                        bl = blocks[nb]
                        for m in tiles[i % CPB]:
                            mm = conv_tile(bl["g"], bl["blk"], m, bl["slot"], bl["ready"])
                        if i % CPB == CPB - 1:
                            flush_silu()
                        if bl["blk"] == NBLK - 1 and bl["g"] + 1 < GROUPS:
                            w_free["conv"] = [mm]
                            if i % CPB == 1:
                                load_conv_x(bl["g"] + 1)
                            if i % CPB == 3:
                                load_conv_bc(bl["g"] + 1)
                if 1 <= i < n + 1:
                    gated_stage(chunks[i - 1])
            w_free["conv"] = [(k["mm_conv"], k["mm_conv"].n)]
            xn_free = [(k["mm_conv"], k["mm_conv"].n), (k["mm_gate"], k["mm_gate"].n)]
            prefix_dt.free = [(k["cs"], k["cs"].n), (k["dtx"], k["dtx"].n), (k["st_tot"], k["st_tot"].n)]
            total_bc.free = [(k["sdec"], k["sdec"].n)]
        q.wait("sync", [(k["stored"], k["stored"].n), (k["st_dec"], k["st_dec"].n), (k["st_tot"], k["st_tot"].n)]
               + [(m, m.n) for m in ffn_stored])

        block = ctx.enter_context(nc.Block())

        @block.sync
        def _(e):
            q.play("sync", e)

        @block.scalar
        def _(e):
            q.play("scalar", e)

        @block.vector
        def _(e):
            q.play("vector", e)

        @block.gpsimd
        def _(e):
            q.play("gpsimd", e)

        @block.tensor
        def _(e):
            q.play("tensor", e)


def kernel(L0_attn_hidden_states, L0_attn_in_proj_w, L0_attn_conv_weight, L0_attn_conv_bias, L0_attn_dt_bias,
           L0_attn_A_log, L0_attn_D, L0_attn_norm_weight, L0_attn_out_proj_w, L0_ffn_lora_A, L0_ffn_lora_B,
           L0_ffn_W, L0_ffn_bias, L0_ffn_lora_weights):
    import numpy as np
    import concourse.bacc as bacc
    from concourse.bass_utils import run_bass_kernel_spmd

    lay = np.ascontiguousarray
    arrays = {
        "hidden": lay(L0_attn_hidden_states),
        "w_in_t": lay(np.asarray(L0_attn_in_proj_w).T),
        "conv_w": lay(np.asarray(L0_attn_conv_weight).reshape(CONV // P, P, TAPS).transpose(1, 0, 2)),
        "conv_b": lay(np.asarray(L0_attn_conv_bias).reshape(CONV // P, P).T),
        "dt_bias": lay(L0_attn_dt_bias).reshape(HEADS, 1),
        "a_log": lay(L0_attn_A_log).reshape(HEADS, 1),
        "d_skip": lay(L0_attn_D),
        "norm_w": lay(np.asarray(L0_attn_norm_weight).reshape(INNER // P, P).T),
        "w_out_t": lay(np.asarray(L0_attn_out_proj_w).T),
        "lora_a": lay(L0_ffn_lora_A).reshape(LORA_N * LORA_R, DM),
        "lora_b_t": lay(np.asarray(L0_ffn_lora_B).transpose(0, 2, 1)).reshape(LORA_N * LORA_R, DM),
        "w_ffn_t": lay(np.asarray(L0_ffn_W).T),
        "ffn_bias": lay(L0_ffn_bias),
        "lora_w": lay(np.repeat(np.asarray(L0_ffn_lora_weights), LORA_R)).reshape(LORA_N * LORA_R, 1),
    }
    nc = bacc.Bacc("TRN2", target_bir_lowering=False, num_devices=1)
    args = [nc.dram_tensor(name, a.shape, mybir.dt.from_np(a.dtype), kind="ExternalInput").ap()
            for name, a in arrays.items()]
    out = nc.dram_tensor("out", (BATCH, SEQ, DM), F32, kind="ExternalOutput").ap()
    build(nc, *args, out)
    r = run_bass_kernel_spmd(nc, [arrays], core_ids=[0])
    return r.results[0]["out"]
```

```python
from contextlib import ExitStack

import concourse.bass as bass
from concourse import mybir

F32 = mybir.dt.float32
F32R = mybir.dt.float32r
ALU = mybir.AluOpType
ACT = mybir.ActivationFunctionType

P = 128
BATCH, SEQ, DM = 2, 1024, 512
HEADS, HD, NS, GROUPS, TAPS = 64, 64, 128, 8, 4
INNER = HEADS * HD
GC = INNER // GROUPS
GH = HEADS // GROUPS
CONV = INNER + 2 * GROUPS * NS
PROJ = INNER + CONV + HEADS
KT = DM // P
XT = GC // P
MT = XT + 2
BLK = 512
NCH = SEQ // P
CPB = BLK // P
NBLK = SEQ // BLK
LORA_N, LORA_R = 8, 16
LORA_SCALE = 32 / 16
EPS = 1e-5
A_LOG_MAX = 88.7
EXP_ZERO = -200.0


class Mark:

    def __init__(self, sem):
        self.sem, self.n = sem, 0


class Slot:

    def __init__(self, buf, mark=None):
        self.buf, self.mark, self.free = buf, mark, []


class Ring:
    def __init__(self, slots):
        self.slots, self.at = slots, -1

    def take(self):
        self.at = (self.at + 1) % len(self.slots)
        return self.slots[self.at]


class Queues:

    def __init__(self):
        self.steps = {k: [] for k in ("tensor", "vector", "scalar", "gpsimd", "sync")}
        self.seen = {k: {} for k in self.steps}

    def do(self, engine, step, after=(), mark=None, by=1):
        for m, n in after:
            if self.seen[engine].get(m, 0) < n:
                self.seen[engine][m] = n
                self.steps[engine].append(lambda e, m=m, n=n: e.wait_ge(m.sem, n))
        if mark is None:
            self.steps[engine].append(step)
            return None
        mark.n += by
        self.steps[engine].append(lambda e: step(e).then_inc(mark.sem, by))
        return mark, mark.n

    def wait(self, engine, after):
        self.do(engine, lambda e: None, after)

    def play(self, engine, e):
        for step in self.steps[engine]:
            step(e)


def build(nc, hidden, w_in_t, conv_w, conv_b, dt_bias, a_log, d_skip, norm_w, w_out_t,
          lora_a, lora_b_t, w_ffn_t, ffn_bias, lora_w, out):
    ctx = ExitStack()
    with ctx:
        def sb(name, shape, dt=F32):
            return ctx.enter_context(nc.sbuf_tensor(name, shape, dt))

        def mark(name):
            return Mark(ctx.enter_context(nc.semaphore(name)))

        def dma_slots(name, shape, n):
            return [Slot(sb(f"{name}{i}", shape), mark(f"landed_{name}{i}")) for i in range(n)]

        q = Queues()
        do = q.do

        decays_d = nc.dram_tensor("decays_d", [BATCH, NCH, HEADS, P], F32).ap()
        totals_d = nc.dram_tensor("totals_d", [BATCH, NCH, HEADS], F32).ap()
        prefix_d = nc.dram_tensor("prefix_d", [P, NCH, P], F32).ap()
        ffn_d = nc.dram_tensor("ffn_d", [BATCH, NCH, P, DM], F32).ap()

        xn_hi = sb("xn_hi", [P, KT, SEQ], F32R)
        xn_lo = sb("xn_lo", [P, KT, SEQ], F32R)
        out_sum = sb("out_sum", [P, NCH, DM])
        wconv_hi = sb("wconv_hi", [P, KT, MT * P], F32R)
        wconv_lo = sb("wconv_lo", [P, KT, MT * P], F32R)
        wgate_hi = sb("wgate_hi", [P, KT, GC], F32R)
        wgate_lo = sb("wgate_lo", [P, KT, GC], F32R)
        wout_hi = sb("wout_hi", [P, XT, DM], F32R)
        wout_lo = sb("wout_lo", [P, XT, DM], F32R)
        stage = dma_slots("stage", [P, KT * GC], 1)[0]
        xc = Ring([Slot(sb(f"xc{i}", [P, MT, BLK])) for i in range(2)])
        halo = Ring([Slot(sb(f"halo{i}", [P, TAPS - 1 + BLK])) for i in range(3)])
        tails = sb("tails", [P, MT, TAPS - 1])
        decay_bc = Ring(dma_slots("decay_bc", [P, GH * P], 2))
        L = Slot(sb("L", [P, GH * P]))
        M = Ring([Slot(sb(f"M{i}", [P, GH * P])) for i in range(2)])
        x_tok = Slot(sb("x_tok", [P, GC]))
        dtx = Ring([Slot(sb(f"dtx{i}", [P, GC])) for i in range(2)])
        skip = Slot(sb("skip", [P, GC]))
        xw = Ring([Slot(sb(f"xw{i}", [P, GC])) for i in range(2)])
        b_tok = Ring([Slot(sb(f"b_tok{i}", [P, NS])) for i in range(2)])
        y = Slot(sb("y", [P, GC]))
        sgate = Slot(sb("sgate", [P, GC]))
        yn = Ring([Slot(sb(f"yn{i}", [P, GC])) for i in range(2)])
        ynt_hi = Slot(sb("ynt_hi", [P, XT, P], F32R))
        ynt_lo = Slot(sb("ynt_lo", [P, XT, P], F32R))
        state = Ring([Slot(sb(f"state{i}", [NS, GC])) for i in range(2)])
        prefix_dt = Slot(sb("prefix_dt", [P, NCH, P]))
        total_bc = Slot(sb("total_bc", [P, NCH * HEADS]))
        prefix_marks = [mark(f"landed_prefix{c}") for c in range(NCH)]
        io = Slot(sb("io", [P, DM]), mark("landed_io"))
        next_x = Slot(sb("next_x", [P, DM])[:, :], mark("landed_next_x"))
        eye8 = sb("eye8", [P, GH, P])
        convw_sb = sb("convw_sb", [P, CONV // P, TAPS])
        convb_sb = sb("convb_sb", [P, CONV // P])
        normw_sb = sb("normw_sb", [P, INNER // P])
        skip_bc = sb("skip_bc", [P, HEADS])
        dtb_sb = sb("dtb_sb", [P, 1])
        nega_sb = sb("nega_sb", [P, 1])
        loraw_sb = sb("loraw_sb", [P, 1])
        half = sb("half", [P, 1])
        stats = sb("stats", [P, NCH, 6])
        mean_var = sb("mean_var", [P, NCH, 2])
        rstd = sb("rstd", [P, NCH])
        square_sum = sb("square_sum", [P, 1])
        mean_square = sb("mean_square", [P, 1])
        rstd_col = sb("rstd_col", [P, 1])
        eye = eye8[:, 0, :]

        def bank(name):
            return ctx.enter_context(nc.psum_tensor(name, [P, 512], F32))

        big = Ring([Slot(bank(f"big{i}")) for i in range(2)])
        turned = Ring([Slot(bank(f"turned{i}")) for i in range(2)])
        ps_g = Slot(bank("ps_g"))
        ps_u = Slot(bank("ps_u"))
        ps_in = Slot(bank("ps_in"))
        ps_cs = Slot(bank("ps_cs"))

        names = """par eye half nega loraw stat mv var rstd norm turn_x hi lo loraB wffn mm_ffn
            ffn_wh ffn_wl biased ffn_act ffn_st mm_dt z absz e u negc lnu ru cru dt da dstart dz
            pfx st_pfx tot mm_pt pt mm_conv h_full h_head h_tail tap0 taps silu
            w_hi w_lo wout_hi wout_lo mm_t mm_bt mm_g xt bt dtx skip scan M xw mm_cs mm_in mm_u mm_gate cs
            y1 y2 sdec state ssq var2 rstd2 sgate yn mm_ynt hi2 lo2 mm_out osum fin1 fin2 fin3
            stored""".split()
        k = {n: mark("s_" + n) for n in names}

        def three_passes(psum, pairs, after, done):
            n = len(pairs) * 3
            i = 0
            for a_hi, a_lo, b_hi, b_lo in pairs:
                for a, b in ((a_hi, b_hi), (a_hi, b_lo), (a_lo, b_hi)):
                    i += 1
                    tok = do("tensor", lambda e, a=a, b=b, i=i: e.matmul(
                        psum, a, b, start=(i == 1), stop=(i == n)),
                        after if i == 1 else (), done if i == n else None)
            return tok

        small = [(convw_sb[:, :, :], conv_w),
                 (convb_sb[:, :], conv_b),
                 (normw_sb[:, :], norm_w),
                 (skip_bc[:, :], d_skip.partition_broadcast(P)),
                 (dtb_sb[0:HEADS, :], dt_bias), (dtb_sb[HEADS:P, :], dt_bias),
                 (nega_sb[0:HEADS, :], a_log), (nega_sb[HEADS:P, :], a_log),
                 (loraw_sb[:, :], lora_w)]
        for dst, src in small:
            params = do("scalar", lambda e, dst=dst, src=src: e.dma_start(dst, src), (), k["par"], 16)
        zeroed = do("gpsimd", lambda e: e.memset(eye8[:, :, :], 0.0), (), k["eye"])
        eye_ready = do("gpsimd", lambda e: e.affine_select(
            out=eye8[:, :, :], in_=eye8[:, :, :], compare_op=ALU.not_equal, fill=1.0, base=0,
            pattern=[[0, GH], [-1, P]], channel_multiplier=1), [zeroed], k["eye"])
        half_ready = do("gpsimd", lambda e: e.memset(half[:, :], -0.5), (), k["half"])
        t = do("vector", lambda e: e.tensor_scalar(nega_sb[:, :], nega_sb[:, :], A_LOG_MAX, None, ALU.min),
               [params], k["nega"])
        t = do("scalar", lambda e: e.activation(nega_sb[:, :], nega_sb[:, :], ACT.Exp), [t], k["nega"])
        nega_ready = do("vector", lambda e: e.tensor_scalar(nega_sb[:, :], nega_sb[:, :], -1.0, None, ALU.mult),
                        [t], k["nega"])
        loraw_ready = do("vector", lambda e: e.tensor_scalar(loraw_sb[:, :], loraw_sb[:, :], LORA_SCALE, None,
                                                             ALU.mult), [params], k["loraw"])

        w_free = {"conv_x": [], "conv_bc": [], "gate": [], "out": []}
        w_ready = {}

        def in_cols(a, n):
            return w_in_t[:, a:a + n].rearrange("(t p) c -> p t c", p=P)

        def weight(kind, g):
            if kind == "conv_x":
                return [(0, in_cols(INNER + g * GC, GC))], wconv_hi[:, :, 0:GC], wconv_lo[:, :, 0:GC]
            if kind == "conv_bc":
                return ([(i * NS, in_cols(2 * INNER + (i * GROUPS + g) * NS, NS)) for i in range(2)],
                        wconv_hi[:, :, GC:MT * P], wconv_lo[:, :, GC:MT * P])
            if kind == "gate":
                return [(0, in_cols(g * GC, GC))], wgate_hi[:, :, :], wgate_lo[:, :, :]
            if kind == "out":
                return ([(0, w_out_t[g * GC:(g + 1) * GC, :].rearrange("(t p) c -> p t c", p=P))],
                        wout_hi[:, :, :], wout_lo[:, :, :])
            return ([(i * HEADS, in_cols(INNER + CONV, HEADS)) for i in range(2)],
                    wout_hi[:, :, 0:P], wout_lo[:, :, 0:P])

        fetched = {}

        def fetch_weight(kind, g):
            pieces, hi, lo = weight(kind, g)
            cols = sum(src.shape[2] for _, src in pieces)
            raw = stage.buf[:, 0:KT * cols].rearrange("p (t c) -> p t c", t=KT)
            for at, src in pieces:
                landed = do("sync", lambda e, at=at, src=src: e.dma_start(raw[:, :, at:at + src.shape[2]], src),
                            stage.free, stage.mark, 16)
            fetched[kind] = raw, hi, lo, landed, g

        def split_weight(kind):
            raw, hi, lo, landed, g = fetched[kind]
            ready = [landed] + w_free["out" if kind == "dt" else kind]
            if kind != "out":
                h = do("scalar", lambda e: e.activation(hi, raw, ACT.Copy), ready, k["w_hi"])
                l = do("gpsimd", lambda e: e.tensor_tensor(lo, raw, hi.bitcast(F32), ALU.subtract),
                       ready + [h], k["w_lo"])
            else:
                for t in range(XT):
                    scale = normw_sb[:, g * XT + t:g * XT + t + 1]
                    h = do("scalar", lambda e, t=t, scale=scale: e.activation(
                        hi[:, t, :], raw[:, t, :], ACT.Copy, scale=scale), ready + [params], k["wout_hi"])
                    l = do("vector", lambda e, t=t, scale=scale: e.scalar_tensor_tensor(
                        lo[:, t, :], raw[:, t, :], scale, hi[:, t, :].bitcast(F32),
                        ALU.mult, ALU.subtract), ready + [h], k["wout_lo"])
            stage.free = [h, l]
            w_ready[kind] = [h, l]

        xn_ready = [None] * NCH
        xn_read = [[] for _ in range(NCH)]

        norm_used = [[] for _ in range(NCH)]

        def norm_fetch(b, c, tile):
            tile.landed = do("sync", lambda e: e.dma_start(tile.buf, hidden[b, c * P:(c + 1) * P, :]),
                             tile.free, tile.mark, 16)

        def norm_stats(c, tile):
            t = do("vector", lambda e: e.bn_stats(stats[:, c, :], tile.buf), [tile.landed], k["stat"])
            t = do("vector", lambda e: e.bn_aggr(mean_var[:, c, :], stats[:, c, :]), [t] + norm_used[c], k["mv"])
            t = do("gpsimd", lambda e: e.tensor_scalar(rstd[:, c:c + 1], mean_var[:, c, 1:2], EPS, None, ALU.add),
                   [t], k["var"])
            tile.rstd = do("gpsimd", lambda e: e.tensor_tensor(
                rstd[:, c:c + 1], rstd[:, c:c + 1], half[:, :], ALU.pow), [t, half_ready], k["rstd"])

        def norm_apply(c, tile):
            tile.normed = do("vector", lambda e: e.tensor_scalar(
                tile.buf, tile.buf, mean_var[:, c, 0:1], rstd[:, c:c + 1], ALU.subtract, ALU.mult),
                [tile.rstd], k["norm"])
            norm_used[c] = [tile.normed]

        def norm_turn(c, tile):
            ps = turned.take()
            for t in range(KT):
                tr = do("tensor", lambda e, t=t: e.transpose(
                    ps.buf[:, t * P:(t + 1) * P], tile.buf[:, t * P:(t + 1) * P], eye),
                    [tile.normed, eye_ready] + ps.free, k["turn_x"] if t == KT - 1 else None)
            tile.free = [tr]
            src = ps.buf[:, :].rearrange("p (t c) -> p t c", t=KT)
            cols = slice(c * P, (c + 1) * P)
            h = do("scalar", lambda e: e.activation(xn_hi[:, :, cols], src, ACT.Copy), [tr] + xn_read[c], k["hi"])
            l = do("vector", lambda e: e.tensor_tensor(
                xn_lo[:, :, cols], src, xn_hi[:, :, cols].bitcast(F32), ALU.subtract), [h] + xn_read[c], k["lo"])
            ps.free = [l]
            xn_ready[c] = [h, l]

        def step_sizes(b):
            zs, es, us, ds = (s.buf for s in (L, M.slots[0], M.slots[1], decay_bc.slots[0]))
            free = L.free + M.slots[0].free + M.slots[1].free + decay_bc.slots[0].free
            hi, lo = wout_hi, wout_lo
            for j in range(NBLK):
                cols = slice(j * BLK, (j + 1) * BLK)
                ps = big.take()
                mm = three_passes(ps.buf[:, :], [(hi[:, t, 0:P], lo[:, t, 0:P], xn_hi[:, t, cols],
                                                  xn_lo[:, t, cols]) for t in range(KT)],
                                  w_ready["dt"] + block_ready(j) + ps.free, k["mm_dt"])
                z = do("scalar", lambda e, ps=ps, cols=cols: e.activation(
                    zs[:, cols], ps.buf[:, :], ACT.Identity, bias=dtb_sb[:, 0:1]), [mm, params] + free, k["z"])
                ps.free = [z]
                for c in range(j * CPB, (j + 1) * CPB):
                    xn_read[c] = [mm]
            w_free["out"] = [mm]
            t = do("vector", lambda e: e.scalar_tensor_tensor(es[:, :], zs[:, :], -1.0, zs[:, :],
                                                              ALU.mult, ALU.min), [z] + free, k["absz"])
            t = do("scalar", lambda e: e.activation(es[:, :], es[:, :], ACT.Exp), [t], k["e"])
            yield
            u = do("vector", lambda e: e.tensor_scalar(us[:, :], es[:, :], 1.0, None, ALU.add), [t] + free, k["u"])
            neg_c = do("vector", lambda e: e.scalar_tensor_tensor(es[:, :], us[:, :], -1.0, es[:, :],
                                                                  ALU.add, ALU.subtract), [u], k["negc"])
            ln = do("scalar", lambda e: e.activation(ds[:, :], us[:, :], ACT.Ln), [u] + free, k["lnu"])
            yield
            t = do("vector", lambda e: e.reciprocal(us[:, :], us[:, :]), [ln, neg_c], k["ru"])
            t = do("vector", lambda e: e.tensor_tensor(es[:, :], es[:, :], us[:, :], ALU.mult), [t], k["cru"])
            yield
            t = do("vector", lambda e: e.tensor_tensor(ds[:, :], ds[:, :], es[:, :], ALU.subtract), [t, ln], k["dt"])
            dt = do("vector", lambda e: e.scalar_tensor_tensor(ds[:, :], zs[:, :], 0.0, ds[:, :],
                                                               ALU.max, ALU.add), [t], k["dt"])
            t = do("vector", lambda e: e.tensor_scalar(us[:, :], ds[:, :], nega_sb[:, 0:1], EXP_ZERO,
                                                       ALU.mult, ALU.max), [dt, nega_ready], k["da"])
            da = do("scalar", lambda e: e.activation(us[:, :], us[:, :], ACT.Exp), [t], k["da"])
            yield
            heads = slice(0, HEADS)
            starts = lambda buf: buf[:, :].rearrange("p (c i) -> p c i", i=P)[heads, :, 0:1]
            t1 = do("vector", lambda e: e.memset(zs[:, :], 0.0), [dt], k["dstart"])
            t0 = do("vector", lambda e: e.tensor_copy(es[:, :], us[:, :]), [da], k["dz"])
            dz = do("vector", lambda e: e.memset(starts(es), 0.0), [t0], k["dz"])
            d1 = do("vector", lambda e: e.tensor_copy(starts(zs), starts(us)), [t1, da], k["dstart"])
            yield
            pfx = do("vector", lambda e: e.tensor_tensor_scan(ds[heads, :], es[heads, :], zs[heads, :], 0.0,
                                                              ALU.mult, ALU.add), [dz, d1, da], k["pfx"])
            std = do("sync", lambda e: e.dma_start(
                decays_d[b].rearrange("c h i -> h c i"),
                es[heads, :].rearrange("h (c i) -> h c i", i=P)), [dz], decays_marks[b], 16)
            yield
            for j in range(2):
                ps = turned.take()
                for i in range(4):
                    mm = do("tensor", lambda e, i=i, j=j, ps=ps: e.transpose(
                        ps.buf[:, i * P:(i + 1) * P], ds[:, (4 * j + i) * P:(4 * j + i + 1) * P], eye),
                        [pfx] + ps.free, k["mm_pt"] if i == 3 else None)
                cp = do("scalar", lambda e, j=j, ps=ps: e.activation(
                    prefix_dt.buf[:, 4 * j:4 * j + 4, :], ps.buf[:, :].rearrange("p (c i) -> p c i", i=P),
                    ACT.Copy), [mm] + prefix_dt.free, k["pt"])
                ps.free = [cp]
            stt = do("sync", lambda e: e.dma_start(totals_d[b:b + 1], prefix_dt.buf[P - 1:P, :, 0:HEADS]),
                     [cp], totals_marks[b], 16)
            if b > 0:
                stp = do("sync", lambda e: e.dma_start(prefix_d, prefix_dt.buf[:, :, :]), [cp],
                         k["st_pfx"], 16)
                prefix_dt.free = [stt, stp]
            else:
                do("sync", lambda e: e.dma_start(
                    total_bc.buf[:, :], totals_d[b].rearrange("c h -> (c h)").partition_broadcast(P)),
                    [stt], k["tot"], 16)
            L.free = [pfx]
            M.slots[0].free = [pfx, std]
            M.slots[1].free = [d1, da]
            decay_bc.slots[0].free = [mm]
            decays_stored[b] = [std]
            prefix_ready[b] = [[cp, (k["tot"], k["tot"].n)]] * NCH

        decays_stored, prefix_ready = [None] * BATCH, [None] * BATCH
        decays_marks = [mark(f"st_decays{b}") for b in range(BATCH)]
        totals_marks = [mark(f"st_totals{b}") for b in range(BATCH)]

        def block_ready(j):
            return [m for c in range(j * CPB, (j + 1) * CPB) for m in xn_ready[c]]

        def reload_prefix(c):
            m = prefix_marks[c]
            hs = slice(c * HEADS, (c + 1) * HEADS)
            used = [(k[n], k[n].n) for n in ("cs", "dtx", "sdec")]
            do("sync", lambda e: e.dma_start(prefix_dt.buf[:, c, :], prefix_d[:, c, :]),
               used + [(k["st_pfx"], k["st_pfx"].n)], m, 16)
            t = do("sync", lambda e: e.dma_start(total_bc.buf[:, hs], totals_d[1, c].partition_broadcast(P)),
                   used + [(totals_marks[1], totals_marks[1].n)], m, 16)
            prefix_ready[1][c] = [t]

        scratch = xc.slots[1].buf[:, :, :].rearrange("p m c -> p (m c)")
        lora_a_sb, lora_b_sb, lora_bs_sb, bias_sb = (scratch[:, i * DM:(i + 1) * DM] for i in range(4))

        def ffn_weights():
            for dst, src in ((lora_a_sb, lora_a), (lora_b_sb, lora_b_t), (bias_sb, ffn_bias.partition_broadcast(P))):
                got = do("sync", lambda e, dst=dst, src=src: e.dma_start(dst, src), (), k["wffn"], 16)
            raw = stage.buf[:, :].rearrange("p (t c) -> p t c", t=KT)
            landed = do("sync", lambda e: e.dma_start(raw, w_ffn_t.rearrange("(t p) c -> p t c", p=P)),
                        stage.free, stage.mark, 16)
            scaled = do("vector", lambda e: e.tensor_scalar(lora_bs_sb, lora_b_sb, loraw_sb[:, 0:1], None,
                                                            ALU.mult), [got, loraw_ready], k["loraB"])
            for t in range(KT):
                ps = big.take()
                mm = do("tensor", lambda e, t=t, ps=ps: e.matmul(
                    ps.buf[:, :], lora_a_sb[:, t * P:(t + 1) * P], lora_bs_sb, start=True, stop=True),
                    [scaled, got] + ps.free, k["mm_ffn"])
                w = do("vector", lambda e, t=t, ps=ps: e.tensor_tensor(
                    raw[:, t, :], raw[:, t, :], ps.buf[:, :], ALU.add), [mm, landed], k["ffn_wl"])
                ps.free = [w]
                h = do("scalar", lambda e, t=t: e.activation(wgate_hi[:, t, :], raw[:, t, :], ACT.Copy),
                       [w], k["ffn_wh"])
                l = do("vector", lambda e, t=t: e.tensor_tensor(
                    wgate_lo[:, t, :], raw[:, t, :], wgate_hi[:, t, :].bitcast(F32), ALU.subtract),
                    [h], k["ffn_wl"])
            stage.free = [h, l]
            w_ready["ffn"] = [h, l, got]

        ffn_out = Ring([sgate, x_tok])
        ffn_stored = [mark("ffn_stored0"), mark("ffn_stored1")]

        def ffn_chunk(b, c):
            cols = slice(c * P, (c + 1) * P)
            ps = big.take()
            mm = three_passes(ps.buf[:, :], [(xn_hi[:, t, cols], xn_lo[:, t, cols], wgate_hi[:, t, :],
                                              wgate_lo[:, t, :]) for t in range(KT)],
                              w_ready["ffn"] + xn_ready[c] + ps.free, k["mm_ffn"])
            bd = do("vector", lambda e: e.tensor_tensor(y.buf[:, :], ps.buf[:, :], bias_sb, ALU.add),
                    [mm] + y.free, k["biased"])
            ps.free = [bd]
            o = ffn_out.take()
            a = do("scalar", lambda e: e.activation(o.buf[:, :], y.buf[:, :], ACT.Silu), [bd] + o.free, k["ffn_act"])
            y.free = [a]
            o.free = [do("sync", lambda e: e.dma_start(ffn_d[b, c], o.buf[:, :]), [a], ffn_stored[c % 2], 16)]
            xn_read[c] = [mm]
            w_free["gate"] = [mm]
            xc.slots[1].free = [bd]

        tail_ready = [None] * MT
        pending_taps = []

        def finish_taps(keep=0):
            while len(pending_taps) > keep:
                pending_taps.pop(0)()

        def conv_tile(g, blk, m, slot, ready):
            tile = g * XT + m if m < XT else INNER // P + (m - XT) * GROUPS + g
            cols = slice(blk * BLK, (blk + 1) * BLK)
            mc = slice(m * P, (m + 1) * P)
            ps = big.take()
            mm = three_passes(ps.buf[:, :], [(wconv_hi[:, t, mc], wconv_lo[:, t, mc], xn_hi[:, t, cols],
                                              xn_lo[:, t, cols]) for t in range(KT)],
                              w_ready["conv_x" if m < XT else "conv_bc"] + block_ready(blk) + ps.free, k["mm_conv"])
            h = halo.take()
            hb, acc = h.buf, slot.buf[:, m, :]
            full = do("scalar", lambda e: e.activation(hb[:, TAPS - 1:], ps.buf[:, :], ACT.Copy),
                      [mm] + h.free, k["h_full"])
            t0 = do("scalar", lambda e: e.activation(
                acc, ps.buf[:, :], ACT.Identity, bias=convb_sb[:, tile:tile + 1],
                scale=convw_sb[:, tile, TAPS - 1:TAPS]), [params] + slot.free, k["tap0"])
            ps.free = [t0, full]
            if blk == 0:
                head = do("gpsimd", lambda e: e.memset(hb[:, 0:TAPS - 1], 0.0), h.free, k["h_head"])
            else:
                head = do("gpsimd", lambda e: e.tensor_copy(hb[:, 0:TAPS - 1], tails[:, m, :]),
                          h.free + [tail_ready[m]], k["h_head"])
            h.free = []
            if blk < NBLK - 1:
                tail_ready[m] = do("gpsimd", lambda e: e.tensor_copy(tails[:, m, :], hb[:, BLK:]),
                                   [full, head], k["h_tail"])
                h.free = [tail_ready[m]]

            def taps():
                tok = t0
                for i in range(TAPS - 1):
                    tok = do("vector", lambda e, i=i: e.scalar_tensor_tensor(
                        acc, hb[:, i:i + BLK], convw_sb[:, tile, i:i + 1], acc, ALU.mult, ALU.add),
                        [tok, full, head], k["taps"])
                h.free = h.free + [tok]
                ready[m] = do("scalar", lambda e: e.activation(acc, acc, ACT.Silu), [tok], k["silu"])

            pending_taps.append(taps)
            return mm

        def heads_bc(ap, n=HD):
            return ap.unsqueeze(2).to_broadcast([P, GH, n])

        def by_head(ap):
            return ap.rearrange("p (h c) -> p h c", h=GH)

        def fetch_decays(ch):
            b, g, c = ch["b"], ch["g"], ch["c"]
            d = ch["decay"] = decay_bc.take()
            src = decays_d[b, c, g * GH:(g + 1) * GH, :].rearrange("h i -> (h i)").partition_broadcast(P)
            ch["landed"] = do("sync", lambda e: e.dma_start(d.buf[:, :], src),
                              d.free + decays_stored[b], d.mark, 16)

        def load_stage(ch):
            g, c, slot, ready = ch["g"], ch["c"], ch["slot"], ch["ready"]
            cc = slice((c % CPB) * P, (c % CPB + 1) * P)
            ps = turned.take()
            for m in range(XT):
                tr = do("tensor", lambda e, m=m: e.transpose(
                    ps.buf[:, m * P:(m + 1) * P], slot.buf[:, m, cc], eye),
                    [ready[m], eye_ready] + ps.free, k["mm_t"] if m == XT - 1 else None)
            xt = do("scalar", lambda e: e.activation(x_tok.buf[:, :], ps.buf[:, :], ACT.Copy),
                    [tr] + x_tok.free, k["xt"])
            ps.free = [xt]
            dt_cols = prefix_dt.buf[:, c, HEADS + g * GH:HEADS + (g + 1) * GH]
            dx = ch["dtx"] = dtx.take()
            ch["dtx_t"] = do("vector", lambda e: e.tensor_tensor(
                by_head(dx.buf[:, :]), by_head(x_tok.buf[:, :]), heads_bc(dt_cols), ALU.mult),
                [xt] + prefix_ready[ch["b"]][c] + dx.free, k["dtx"])
            ch["xt"] = xt
            d = ch["decay"]
            sc = do("vector", lambda e: e.tensor_tensor_scan(
                L.buf[:, :], d.buf[:, :], eye8[:, :, :].rearrange("p h i -> p (h i)"), 0.0,
                ALU.mult, ALU.add), [ch["landed"], eye_ready] + L.free, k["scan"])
            d.free = [sc]
            L.free = [sc]
            if c < NCH - 1:
                w = ch["xw"] = xw.take()
                ch["xw_t"] = do("vector", lambda e: e.tensor_tensor(
                    by_head(w.buf[:, :]), by_head(dx.buf[:, :]),
                    by_head(L.buf[:, :])[:, :, P - 1:P].to_broadcast([P, GH, HD]), ALU.mult),
                    [ch["dtx_t"], sc] + w.free, k["xw"])
                L.free = [ch["xw_t"]]
            ch["scan"] = sc

        def mask_stage(ch):
            c, slot, ready = ch["c"], ch["slot"], ch["ready"]
            cc = slice((c % CPB) * P, (c % CPB + 1) * P)
            if c < NCH - 1:
                bt = do("tensor", lambda e: e.transpose(ps_u.buf[:, 0:P], slot.buf[:, XT, cc], eye),
                        [ready[XT]] + ps_u.free, k["mm_bt"])
                b_ = ch["b_tok"] = b_tok.take()
                ch["bt"] = do("scalar", lambda e: e.activation(b_.buf[:, :], ps_u.buf[:, 0:P], ACT.Copy),
                              [bt] + b_.free, k["bt"])
                ps_u.free = [ch["bt"]]
            gm = do("tensor", lambda e: e.matmul(ps_g.buf[:, 0:P], slot.buf[:, XT, cc], slot.buf[:, XT + 1, cc],
                                                 start=True, stop=True),
                    [ready[XT], ready[XT + 1]] + ps_g.free, k["mm_g"])
            mx = ch["M"] = M.take()
            ch["M_t"] = do("vector", lambda e: e.tensor_tensor(
                by_head(mx.buf[:, :]), by_head(L.buf[:, :]),
                ps_g.buf[:, 0:P].unsqueeze(1).to_broadcast([P, GH, P]), ALU.mult),
                [ch["scan"], gm] + mx.free, k["M"])
            ps_g.free = [ch["M_t"]]
            L.free = L.free + [ch["M_t"]]

        def skip_stage(ch):
            g = ch["g"]
            ch["skip_t"] = do("gpsimd", lambda e: e.tensor_tensor(
                by_head(skip.buf[:, :]), by_head(x_tok.buf[:, :]),
                heads_bc(skip_bc[:, g * GH:(g + 1) * GH]), ALU.mult), [ch["xt"], params] + skip.free, k["skip"])
            x_tok.free = [ch["dtx_t"], ch["skip_t"]]

        def gate_stage(ch):
            c = ch["c"]
            cols = slice(c * P, (c + 1) * P)
            ps = big.take()
            mm = three_passes(ps.buf[:, :], [(xn_hi[:, t, cols], xn_lo[:, t, cols], wgate_hi[:, t, :],
                                              wgate_lo[:, t, :]) for t in range(KT)],
                              w_ready["gate"] + xn_ready[c] + ps.free, k["mm_gate"])
            w_free["gate"] = [mm]
            xn_read[c] = [mm, last_conv[c // CPB]]
            ch["sgate_t"] = do("scalar", lambda e: e.activation(sgate.buf[:, :], ps.buf[:, :], ACT.Silu),
                               [mm] + sgate.free, k["sgate"])
            ps.free = [ch["sgate_t"]]

        def mix_stage(ch):
            g, c, slot = ch["g"], ch["c"], ch["slot"]
            cc = slice((c % CPB) * P, (c % CPB + 1) * P)
            dx, mx = ch["dtx"], ch["M"]
            tok = None
            if c > 0:
                s = ch["state_in"]
                tok = do("tensor", lambda e: e.matmul(ps_cs.buf[:, :], slot.buf[:, XT + 1, cc], s.buf[:, :],
                                                      start=True, stop=True),
                         [ch["state_t"]] + ps_cs.free, k["mm_cs"])
            for h in range(GH):
                n = 2 * HD if h < GH - 1 else HD
                mi = do("tensor", lambda e, h=h, n=n: e.matmul(
                    ps_in.buf[:, h * HD:h * HD + n], mx.buf[:, h * P:(h + 1) * P],
                    dx.buf[:, h * HD:h * HD + n], start=True, stop=True, skip_group_check=True),
                    [ch["M_t"], ch["dtx_t"]] + ps_in.free, k["mm_in"] if h == GH - 1 else None)
            dx.free, mx.free = [mi], [mi]
            if c < NCH - 1:
                w, b_ = ch["xw"], ch["b_tok"]
                mu = do("tensor", lambda e: e.matmul(ps_u.buf[:, :], b_.buf[:, :], w.buf[:, :],
                                                     start=True, stop=True),
                        [ch["xw_t"], ch["bt"]] + ps_u.free, k["mm_u"])
                w.free, b_.free = [mu], [mu]
            ch["last_pe"] = mi
            if c > 0:
                cs = do("vector", lambda e: e.tensor_tensor(
                    by_head(y.buf[:, :]), by_head(ps_cs.buf[:, :]),
                    heads_bc(prefix_dt.buf[:, c, g * GH:(g + 1) * GH]), ALU.mult),
                    [tok] + prefix_ready[ch["b"]][c] + y.free, k["cs"])
                ps_cs.free = [cs]
                y1 = do("vector", lambda e: e.tensor_tensor(y.buf[:, :], ps_in.buf[:, :], y.buf[:, :], ALU.add),
                        [mi, cs], k["y1"])
                ps_in.free = [y1]
            if c < NCH - 1:
                if c > 0:
                    new = ch["state_out"]
                    st = do("vector", lambda e: e.tensor_tensor(
                        new.buf[:, :], ps_u.buf[:, :], new.buf[:, :], ALU.add), [mu, ch["sdec_t"]], k["state"])
                else:
                    new = state.take()
                    st = do("vector", lambda e: e.tensor_copy(new.buf[:, :], ps_u.buf[:, :]),
                            [mu] + new.free, k["state"])
                ps_u.free = [st]
                ch["next"]["state_in"], ch["next"]["state_t"] = new, st
            if c > 0:
                y2 = do("vector", lambda e: e.tensor_tensor(y.buf[:, :], y.buf[:, :], skip.buf[:, :], ALU.add),
                        [y1, ch["skip_t"]], k["y2"])
            else:
                y2 = do("vector", lambda e: e.tensor_tensor(y.buf[:, :], ps_in.buf[:, :], skip.buf[:, :], ALU.add),
                        [mi, ch["skip_t"]] + y.free, k["y2"])
                ps_in.free = [y2]
            skip.free = [y2]
            ch["y2"] = y2
            if c > 0:
                ch["state_in"].free = ch["state_in"].free + [tok]
            if 0 < c + 1 < NCH - 1:
                tot = total_bc.buf[:, (c + 1) * HEADS + g * GH:(c + 1) * HEADS + (g + 1) * GH]
                dec = ch["next"]["state_out"] = state.take()
                ch["next"]["sdec_t"] = do("gpsimd", lambda e: e.tensor_tensor(
                    by_head(dec.buf[:, :]), by_head(new.buf[:, :]), heads_bc(tot), ALU.mult),
                    [st] + prefix_ready[ch["b"]][c + 1] + dec.free, k["sdec"])
                new.free = [ch["next"]["sdec_t"]]
            elif c < NCH - 1:
                new.free = []

        def norm_stage(ch):
            n_ = ch["yn"] = yn.take()
            sq = do("scalar", lambda e: e.activation(n_.buf[:, :], y.buf[:, :], ACT.Square,
                                                     accum_out=square_sum[:, :]),
                    [ch["y2"]] + n_.free + [(k["rstd2"], k["rstd2"].n)], k["ssq"])
            v = do("gpsimd", lambda e: e.tensor_scalar(mean_square[:, :], square_sum[:, :], 1.0 / GC, EPS, ALU.mult, ALU.add),
                   [sq], k["var2"])
            ch["rstd_t"] = do("gpsimd", lambda e: e.tensor_tensor(rstd_col[:, :], mean_square[:, :], half[:, :], ALU.pow),
                              [v, half_ready, (k["yn"], k["yn"].n)], k["rstd2"])

        def gated_stage(ch):
            ch["yn_t"] = do("vector", lambda e: e.scalar_tensor_tensor(
                ch["yn"].buf[:, :], y.buf[:, :], rstd_col[:, 0:1], sgate.buf[:, :], ALU.mult, ALU.mult),
                [ch["rstd_t"], ch["sgate_t"]], k["yn"])
            y.free = [ch["yn_t"]]
            sgate.free = [ch["yn_t"]]

        def turn_stage(ch):
            ps = turned.take()
            for t in range(XT):
                tr = do("tensor", lambda e, t=t: e.transpose(
                    ps.buf[:, t * P:(t + 1) * P], ch["yn"].buf[:, t * P:(t + 1) * P], eye),
                    [ch["yn_t"]] + ps.free, k["mm_ynt"] if t == XT - 1 else None)
            ch["yn"].free = [tr]
            src = ps.buf[:, :].rearrange("p (t c) -> p t c", t=XT)
            h = do("scalar", lambda e: e.activation(ynt_hi.buf[:, :, :], src, ACT.Copy),
                   [tr] + ynt_hi.free, k["hi2"])
            l = do("vector", lambda e: e.tensor_tensor(ynt_lo.buf[:, :, :], src, ynt_hi.buf[:, :, :].bitcast(F32),
                                                       ALU.subtract), [h] + ynt_lo.free, k["lo2"])
            ps.free = [l]
            ch["ynt"] = [h, l]

        def project_stage(ch):
            b, g, c = ch["b"], ch["g"], ch["c"]
            ps = big.take()
            mm = three_passes(ps.buf[:, :], [(ynt_hi.buf[:, t, :], ynt_lo.buf[:, t, :], wout_hi[:, t, :],
                                              wout_lo[:, t, :]) for t in range(XT)],
                              w_ready["out"] + ch["ynt"] + ps.free, k["mm_out"])
            ynt_hi.free = ynt_lo.free = [mm]
            w_free["out"] = [mm]
            acc = out_sum[:, c, :]
            if g == 0:
                o = do("vector", lambda e: e.tensor_copy(acc, ps.buf[:, :]), [mm] + stored[c], k["osum"])
            else:
                o = do("vector", lambda e: e.tensor_tensor(acc, acc, ps.buf[:, :], ALU.add),
                       [mm, sum_ready[c]], k["osum"])
            ps.free = [o]
            sum_ready[c] = o
            if g == GROUPS - 1:
                lf = do("sync", lambda e: e.dma_start(io.buf[:, :], ffn_d[b, c]),
                        io.free + [(m, m.n) for m in ffn_stored], io.mark, 16)
                f = do("gpsimd", lambda e: e.tensor_tensor(acc, acc, io.buf[:, :], ALU.mult), [o, lf], k["fin1"])
                lx = do("sync", lambda e: e.dma_start(io.buf[:, :], hidden[b, c * P:(c + 1) * P, :]),
                        [f], io.mark, 16)
                f = do("gpsimd", lambda e: e.tensor_tensor(acc, acc, io.buf[:, :], ALU.add), [f, lx], k["fin2"])
                io.free = [f]
                stored[c] = [do("sync", lambda e: e.dma_start(out[b, c * P:(c + 1) * P, :], acc), [f],
                                k["stored"], 16)]

        stored = [[] for _ in range(NCH)]
        sum_ready = [None] * NCH

        early_x = [Slot(out_sum[:, c, :], mark(f"landed_x{c}")) for c in range(NCH)]
        fetch_weight("dt", 0)
        for c in range(NCH):
            norm_fetch(1, c, early_x[c])
        split_weight("dt")
        for b in (1, 0):
            if b == 1:
                for c in range(NCH):
                    norm_stats(c, early_x[c])
                    if c > 0:
                        norm_apply(c - 1, early_x[c - 1])
                        norm_turn(c - 1, early_x[c - 1])
                norm_apply(NCH - 1, early_x[NCH - 1])
                norm_turn(NCH - 1, early_x[NCH - 1])
                ffn_weights()
                for c in range(NCH):
                    norm_fetch(0, c, early_x[c])
            chain = step_sizes(b)
            next(chain)
            for c in range(NCH):
                ffn_chunk(b, c)
                if b == 1:
                    norm_stats(c, early_x[c])
                    if c > 0:
                        norm_apply(c - 1, early_x[c - 1])
                        norm_turn(c - 1, early_x[c - 1])
                next(chain, None)
            if b == 1:
                norm_apply(NCH - 1, early_x[NCH - 1])
                norm_turn(NCH - 1, early_x[NCH - 1])
                fetch_weight("conv_x", 0)
                split_weight("conv_x")
                fetch_weight("conv_bc", 0)
                split_weight("conv_bc")
                fetch_weight("gate", 0)
        split_weight("gate")
        fetch_weight("out", 0)
        split_weight("out")
        fetch_weight("conv_x", 1)

        NG = GROUPS * NBLK * BATCH
        last_conv = [None] * NBLK
        blocks, chunks = [], []
        for i in range(NG):
            bl = dict(b=i // (GROUPS * NBLK), g=i // NBLK % GROUPS, blk=i % NBLK, slot=xc.slots[i % 2],
                      ready=[None] * MT)
            blocks.append(bl)
            chunks += [dict(bl, c=bl["blk"] * CPB + j, block=i) for j in range(CPB)]
        for a, nxt in zip(chunks, chunks[1:]):
            a["next"] = nxt
        n = len(chunks)
        early, late = [[], [1], [3], [5]], [[0], [2], [4], []]

        def conv_tiles(nb, tiles):
            if nb == NG:
                return
            bl = blocks[nb]
            for m in tiles:
                mm = conv_tile(bl["g"], bl["blk"], m, bl["slot"], bl["ready"])
                last_conv[bl["blk"]] = mm
                w_free["conv_x" if m < XT else "conv_bc"] = [mm]
                finish_taps(1)

        def swap_weights(i):
            group, at = divmod(i, NCH)
            more = group + 1 < BATCH * GROUPS
            g, nxt = group % GROUPS, (group + 1) % GROUPS
            if at == 0 and group > 0:
                if more:
                    fetch_weight("conv_x", nxt)
                else:
                    fetch_weight("out", g)
            if at == 2 and more:
                split_weight("conv_x")
                if group > 0:
                    fetch_weight("out", g)
                else:
                    fetch_weight("conv_bc", nxt)
            if at == 3 and group > 0:
                if more:
                    fetch_weight("conv_bc", nxt)
            if at == 4 and more:
                split_weight("conv_bc")
                fetch_weight("gate", nxt)

        conv_tiles(0, range(MT))
        finish_taps()
        fetch_decays(chunks[0])
        behind = n // 2 - NCH + 1
        for i in range(n + 4):
            if i + 1 < n:
                fetch_decays(chunks[i + 1])
            if i < n:
                load_stage(chunks[i])
                conv_tiles(chunks[i]["block"] + 1, early[i % CPB])
            if 0 <= i - behind < NCH:
                norm_stats(i - behind, next_x)
            if i >= 4:
                project_stage(chunks[i - 4])
            if i % NCH == 3 and NCH < i < n:
                split_weight("out")
            if 3 <= i < n + 3:
                turn_stage(chunks[i - 3])
            if i < n:
                mask_stage(chunks[i])
            if i % CPB == CPB - 1:
                finish_taps()
            if 0 <= i - behind < NCH:
                norm_apply(i - behind, next_x)
            if 1 <= i < n + 1:
                ch = chunks[i - 1]
                gate_stage(ch)
                if i % NCH == 0 and i < n:
                    split_weight("gate")
                mix_stage(ch)
                norm_stage(ch)
                if ch["c"] % CPB == CPB - 1:
                    ch["slot"].free = [ch["last_pe"]]
            if 0 <= i - behind < NCH:
                norm_turn(i - behind, next_x)
                reload_prefix(i - behind)
            if 0 <= i + 1 - behind < NCH:
                norm_fetch(1, i + 1 - behind, next_x)
            if i < n:
                skip_stage(chunks[i])
                conv_tiles(chunks[i]["block"] + 1, late[i % CPB])
            if 1 <= i < n + 1:
                gated_stage(chunks[i - 1])
            if i < n:
                swap_weights(i)
        q.wait("sync", [(m, m.n) for m in [k["stored"], k["st_pfx"]] + decays_marks + totals_marks + ffn_stored])

        block = ctx.enter_context(nc.Block())

        @block.sync
        def _(e):
            q.play("sync", e)

        @block.scalar
        def _(e):
            q.play("scalar", e)

        @block.vector
        def _(e):
            q.play("vector", e)

        @block.gpsimd
        def _(e):
            q.play("gpsimd", e)

        @block.tensor
        def _(e):
            q.play("tensor", e)


def kernel(L0_attn_hidden_states, L0_attn_in_proj_w, L0_attn_conv_weight, L0_attn_conv_bias, L0_attn_dt_bias,
           L0_attn_A_log, L0_attn_D, L0_attn_norm_weight, L0_attn_out_proj_w, L0_ffn_lora_A, L0_ffn_lora_B,
           L0_ffn_W, L0_ffn_bias, L0_ffn_lora_weights):
    import numpy as np
    import concourse.bacc as bacc
    from concourse.bass_utils import run_bass_kernel_spmd

    lay = np.ascontiguousarray
    arrays = {
        "hidden": lay(L0_attn_hidden_states),
        "w_in_t": lay(np.asarray(L0_attn_in_proj_w).T),
        "conv_w": lay(np.asarray(L0_attn_conv_weight).reshape(CONV // P, P, TAPS).transpose(1, 0, 2)),
        "conv_b": lay(np.asarray(L0_attn_conv_bias).reshape(CONV // P, P).T),
        "dt_bias": lay(L0_attn_dt_bias).reshape(HEADS, 1),
        "a_log": lay(L0_attn_A_log).reshape(HEADS, 1),
        "d_skip": lay(L0_attn_D),
        "norm_w": lay(np.asarray(L0_attn_norm_weight).reshape(INNER // P, P).T),
        "w_out_t": lay(np.asarray(L0_attn_out_proj_w).T),
        "lora_a": lay(L0_ffn_lora_A).reshape(LORA_N * LORA_R, DM),
        "lora_b_t": lay(np.asarray(L0_ffn_lora_B).transpose(0, 2, 1)).reshape(LORA_N * LORA_R, DM),
        "w_ffn_t": lay(np.asarray(L0_ffn_W).T),
        "ffn_bias": lay(L0_ffn_bias),
        "lora_w": lay(np.repeat(np.asarray(L0_ffn_lora_weights), LORA_R)).reshape(LORA_N * LORA_R, 1),
    }
    nc = bacc.Bacc("TRN2", target_bir_lowering=False, num_devices=1)
    args = [nc.dram_tensor(name, a.shape, mybir.dt.from_np(a.dtype), kind="ExternalInput").ap()
            for name, a in arrays.items()]
    out = nc.dram_tensor("out", (BATCH, SEQ, DM), F32, kind="ExternalOutput").ap()
    build(nc, *args, out)
    r = run_bass_kernel_spmd(nc, [arrays], core_ids=[0])
    return r.results[0]["out"]
```

```python
from contextlib import ExitStack

import concourse.bass as bass
from concourse import mybir

F32 = mybir.dt.float32
F32R = mybir.dt.float32r
ALU = mybir.AluOpType
ACT = mybir.ActivationFunctionType

P = 128
BATCH, SEQ, DM = 2, 1024, 512
HEADS, HD, NS, GROUPS, TAPS = 64, 64, 128, 8, 4
INNER = HEADS * HD
GC = INNER // GROUPS
GH = HEADS // GROUPS
CONV = INNER + 2 * GROUPS * NS
KT = DM // P
XT = GC // P
MT = XT + 2
BLK = 512
NCH = SEQ // P
CPB = BLK // P
NBLK = SEQ // BLK
LORA_N, LORA_R = 8, 16
LORA_SCALE = 32 / 16
EPS = 1e-5
A_LOG_MAX = 88.7
EXP_ZERO = -200.0


class Mark:

    def __init__(self, sem):
        self.sem, self.n = sem, 0


class Slot:

    def __init__(self, buf, mark=None):
        self.buf, self.mark, self.free = buf, mark, []


class Ring:
    def __init__(self, slots):
        self.slots, self.at = slots, -1

    def take(self):
        self.at = (self.at + 1) % len(self.slots)
        return self.slots[self.at]


class Queues:

    def __init__(self):
        self.steps = {k: [] for k in ("tensor", "vector", "scalar", "gpsimd", "sync")}
        self.seen = {k: {} for k in self.steps}

    def do(self, engine, step, after=(), mark=None, by=1):
        for m, n in after:
            if self.seen[engine].get(m, 0) < n:
                self.seen[engine][m] = n
                self.steps[engine].append(lambda e, m=m, n=n: e.wait_ge(m.sem, n))
        if mark is None:
            self.steps[engine].append(step)
            return None
        mark.n += by
        self.steps[engine].append(lambda e: step(e).then_inc(mark.sem, by))
        return mark, mark.n

    def wait(self, engine, after):
        self.do(engine, lambda e: None, after)

    def play(self, engine, e):
        for step in self.steps[engine]:
            step(e)


def build(nc, hidden, w_in_t, conv_w, conv_b, dt_bias, a_log, d_skip, norm_w, w_out_t,
          lora_a, lora_b_t, w_ffn_t, ffn_bias, lora_w, out):
    ctx = ExitStack()
    with ctx:
        def sb(name, shape, dt=F32):
            return ctx.enter_context(nc.sbuf_tensor(name, shape, dt))

        def mark(name):
            return Mark(ctx.enter_context(nc.semaphore(name)))

        def dma_slots(name, shape, n):
            return [Slot(sb(f"{name}{i}", shape), mark(f"landed_{name}{i}")) for i in range(n)]

        q = Queues()
        do = q.do

        decays_d = nc.dram_tensor("decays_d", [BATCH, NCH, HEADS, P], F32).ap()
        totals_d = nc.dram_tensor("totals_d", [BATCH, NCH, HEADS], F32).ap()
        prefix_d = nc.dram_tensor("prefix_d", [P, NCH, P], F32).ap()
        ffn_d = nc.dram_tensor("ffn_d", [BATCH, NCH, P, DM], F32).ap()

        xn_hi = sb("xn_hi", [P, KT, SEQ], F32R)
        xn_lo = sb("xn_lo", [P, KT, SEQ], F32R)
        out_sum = sb("out_sum", [P, NCH, DM])
        wconv_hi = sb("wconv_hi", [P, KT, MT * P], F32R)
        wconv_lo = sb("wconv_lo", [P, KT, MT * P], F32R)
        wgate_hi = sb("wgate_hi", [P, KT, GC], F32R)
        wgate_lo = sb("wgate_lo", [P, KT, GC], F32R)
        wout_hi = sb("wout_hi", [P, XT, DM], F32R)
        wout_lo = sb("wout_lo", [P, XT, DM], F32R)
        stage = Ring(dma_slots("stage", [P, KT * GC], 2))
        xc = Ring([Slot(sb(f"xc{i}", [P, MT, BLK])) for i in range(2)])
        halo = Ring([Slot(sb(f"halo{i}", [P, TAPS - 1 + BLK])) for i in range(2)])
        tails = sb("tails", [P, MT, TAPS - 1])
        decay = Ring(dma_slots("decay", [P, GH * P], 3))
        x_tok = Slot(sb("x_tok", [P, GC]))
        dtx = Ring([Slot(sb(f"dtx{i}", [P, GC])) for i in range(2)])
        skip = Slot(sb("skip", [P, GC]))
        xw = Slot(sb("xw", [P, GC]))
        xw_hi = Slot(sb("xw_hi", [P, GC], F32R))
        xw_lo = Slot(sb("xw_lo", [P, GC], F32R))
        b_hi = Ring([Slot(sb(f"b_hi{i}", [P, NS], F32R)) for i in range(2)])
        b_lo = Ring([Slot(sb(f"b_lo{i}", [P, NS], F32R)) for i in range(2)])
        y = Slot(sb("y", [P, GC]))
        sgate = Slot(sb("sgate", [P, GC]))
        yn = Ring([Slot(sb(f"yn{i}", [P, GC])) for i in range(2)])
        ynt_hi = Slot(sb("ynt_hi", [P, XT, P], F32R))
        ynt_lo = Slot(sb("ynt_lo", [P, XT, P], F32R))
        state = Ring([Slot(sb(f"state{i}", [NS, GC])) for i in range(2)])
        prefix_dt = Slot(sb("prefix_dt", [P, NCH, P]))
        total_bc = Slot(sb("total_bc", [P, NCH * HEADS]))
        prefix_marks = [mark(f"landed_prefix{c}") for c in range(NCH)]
        io = Slot(sb("io", [P, DM]), mark("landed_io"))
        next_x = Slot(sb("next_x", [P, DM])[:, :], mark("landed_next_x"))
        eye8 = sb("eye8", [P, GH, P])
        convw_sb = sb("convw_sb", [P, CONV // P, TAPS])
        convb_sb = sb("convb_sb", [P, CONV // P])
        normw_sb = sb("normw_sb", [P, INNER // P])
        skip_bc = sb("skip_bc", [P, HEADS])
        dtb_sb = sb("dtb_sb", [P, 1])
        nega_sb = sb("nega_sb", [P, 1])
        loraw_sb = sb("loraw_sb", [P, 1])
        half = sb("half", [P, 1])
        stats = sb("stats", [P, 2, 6])
        mean_var = sb("mean_var", [P, NCH, 2])
        rstd = sb("rstd", [P, NCH])
        square_sum = sb("square_sum", [P, 1])
        mean_square = sb("mean_square", [P, 1])
        rstd_col = sb("rstd_col", [P, 1])
        eye = eye8[:, 0, :]

        def bank(name):
            return ctx.enter_context(nc.psum_tensor(name, [P, 512], F32))

        big = Ring([Slot(bank(f"big{i}")) for i in range(2)])
        turned = Ring([Slot(bank(f"turned{i}")) for i in range(2)])
        ps_g = Slot(bank("ps_g"))
        ps_u = Slot(bank("ps_u"))
        ps_in = Slot(bank("ps_in"))
        ps_cs = Slot(bank("ps_cs"))

        names = """par lora_par eye half nega loraw stat mv var rstd norm turn_x hi lo loraB wffn mm_ffn
            ffn_wh ffn_wl ffn_lo biased ffn_act mm_dt z absz e u negc lnu ru cru dt da dstart dcopy dz
            pfx mm_pt pt mm_conv h_full h_head h_tail tap0 taps silu w_hi w_lo w_lo_dve wout_scaled
            mm_t mm_bt mm_g xt bt dtx skip scan M xw mm_cs mm_in mm_u mm_gate cs y1 y2 sdec state ssq
            var2 rstd2 sgate yn mm_ynt hi2 lo2 mm_out osum fin1 fin2 stored
            bt_lo xw_hi xw_lo""".split()
        k = {n: mark("s_" + n) for n in names}

        def three_passes(psum, a_b, a_ready, b_ready, free, done, a_lo_last=False):
            n = len(a_b) * 3
            i = 0
            rest = [(1, 0, a_ready[1]), (0, 1, b_ready[1])]
            for a_part, b_part, after in [(0, 0, a_ready[0] + b_ready[0] + free)] + rest[::-1 if a_lo_last else 1]:
                for a, b in a_b:
                    i += 1
                    tok = do("tensor", lambda e, a=a[a_part], b=b[b_part], i=i: e.matmul(
                        psum, a, b, start=(i == 1), stop=(i == n)),
                        after, done if i == n else None)
            return tok

        lora_param = do("scalar", lambda e: e.dma_start(loraw_sb[:, :], lora_w), (), k["lora_par"], 16)
        small = [(dtb_sb[0:HEADS, :], dt_bias), (dtb_sb[HEADS:P, :], dt_bias),
                 (nega_sb[0:HEADS, :], a_log), (nega_sb[HEADS:P, :], a_log),
                 (convw_sb[:, :, :], conv_w),
                 (convb_sb[:, :], conv_b),
                 (normw_sb[:, :], norm_w),
                 (skip_bc[:, :], d_skip.partition_broadcast(P))]
        for dst, src in small:
            params = do("scalar", lambda e, dst=dst, src=src: e.dma_start(dst, src), (), k["par"], 16)
        zeroed = do("gpsimd", lambda e: e.memset(eye8[:, :, :], 0.0), (), k["eye"])
        eye_ready = do("gpsimd", lambda e: e.affine_select(
            out=eye8[:, :, :], in_=eye8[:, :, :], compare_op=ALU.not_equal, fill=1.0, base=0,
            pattern=[[0, GH], [-1, P]], channel_multiplier=1), [zeroed], k["eye"])
        half_ready = do("gpsimd", lambda e: e.memset(half[:, :], -0.5), (), k["half"])

        w_free = {"conv_x": [], "conv_bc": [], "gate": [], "out": []}
        w_ready = {}

        def in_cols(a, n):
            return w_in_t[:, a:a + n].rearrange("(t p) c -> p t c", p=P)

        def weight(kind, g):
            if kind == "conv_x":
                return [(0, in_cols(INNER + g * GC, GC))], wconv_hi[:, :, 0:GC], wconv_lo[:, :, 0:GC]
            if kind == "conv_bc":
                return ([(i * NS, in_cols(2 * INNER + (i * GROUPS + g) * NS, NS)) for i in range(2)],
                        wconv_hi[:, :, GC:MT * P], wconv_lo[:, :, GC:MT * P])
            if kind == "gate":
                return [(0, in_cols(g * GC, GC))], wgate_hi[:, :, :], wgate_lo[:, :, :]
            if kind == "out":
                return ([(0, w_out_t[g * GC:(g + 1) * GC, :].rearrange("(t p) c -> p t c", p=P))],
                        wout_hi[:, :, :], wout_lo[:, :, :])
            return ([(i * HEADS, in_cols(INNER + CONV, HEADS)) for i in range(2)],
                    wout_hi[:, :, 0:P], wout_lo[:, :, 0:P])

        fetched, lo_marks = {}, {}

        def fetch_weight(kind, g, room=None):
            room = room or stage.take()
            pieces, hi, lo = weight(kind, g)
            cols = sum(src.shape[2] for _, src in pieces)
            raw = room.buf[:, 0:KT * cols].rearrange("p (t c) -> p t c", t=KT)
            for at, src in pieces:
                landed = do("sync", lambda e, at=at, src=src: e.dma_start(raw[:, :, at:at + src.shape[2]], src),
                            room.free, room.mark, 16)
            fetched[kind] = raw, hi, lo, landed, g, room

        def scale_out_weight():
            raw, hi, lo, landed, g, room = fetched["out"]
            for t in range(XT):
                scaled = do("scalar", lambda e, t=t: e.activation(
                    raw[:, t, :], raw[:, t, :], ACT.Copy, scale=normw_sb[:, g * XT + t:g * XT + t + 1]),
                    [landed, params], k["wout_scaled"])
            fetched["out"] = raw, hi, lo, scaled, g, room

        def split_weight(kind, tiles=range(KT), lo_engines=("gpsimd",) * KT):
            raw, hi, lo, landed, g, room = fetched[kind]
            ready = [landed] + w_free["out" if kind == "dt" else kind]
            done = lo_marks.setdefault((kind, g), {})
            for t in tiles:
                h = do("scalar", lambda e, t=t: e.activation(hi[:, t, :], raw[:, t, :], ACT.Copy),
                       ready, k["w_hi"])
                eng = lo_engines[t]
                done[eng] = do(eng, lambda e, t=t: e.tensor_tensor(
                    lo[:, t, :], raw[:, t, :], hi[:, t, :].bitcast(F32), ALU.subtract),
                    ready + [h], k["w_lo" if eng == "gpsimd" else "w_lo_dve"])
            room.free = [h] + list(done.values())
            w_ready[kind] = [h], list(done.values())

        xn_ready = [None] * NCH
        xn_read = [[] for _ in range(NCH)]

        norm_used = [[] for _ in range(NCH)]

        def norm_fetch(b, c, tile):
            tile.landed = do("sync", lambda e: e.dma_start(tile.buf, hidden[b, c * P:(c + 1) * P, :]),
                             tile.free, tile.mark, 16)

        def norm_stats(c, tile):
            t = do("vector", lambda e: e.bn_stats(stats[:, c % 2, :], tile.buf), [tile.landed], k["stat"])
            t = do("vector", lambda e: e.bn_aggr(mean_var[:, c, :], stats[:, c % 2, :]), [t] + norm_used[c], k["mv"])
            t = do("gpsimd", lambda e: e.tensor_scalar(rstd[:, c:c + 1], mean_var[:, c, 1:2], EPS, None, ALU.add),
                   [t], k["var"])
            tile.rstd = do("gpsimd", lambda e: e.tensor_tensor(
                rstd[:, c:c + 1], rstd[:, c:c + 1], half[:, :], ALU.pow), [t, half_ready], k["rstd"])

        def norm_apply(c, tile):
            tile.normed = do("vector", lambda e: e.tensor_scalar(
                tile.buf, tile.buf, mean_var[:, c, 0:1], rstd[:, c:c + 1], ALU.subtract, ALU.mult),
                [tile.rstd], k["norm"])
            norm_used[c] = [tile.normed]

        def norm_turn(c, tile):
            ps = turned.take()
            for t in range(KT):
                tr = do("tensor", lambda e, t=t: e.transpose(
                    ps.buf[:, t * P:(t + 1) * P], tile.buf[:, t * P:(t + 1) * P], eye),
                    [tile.normed, eye_ready] + ps.free, k["turn_x"] if t == KT - 1 else None)
            tile.free = [tr]
            cols = slice(c * P, (c + 1) * P)
            src = ps.buf[:, :].rearrange("p (t c) -> p t c", t=KT)
            tile.hi = do("scalar", lambda e: e.activation(xn_hi[:, :, cols], src, ACT.Copy), [tr] + xn_read[c],
                         k["hi"])
            tile.turned, ps.free = ps, [tile.hi]

        def norm_split(c, tile):
            h, ps = tile.hi, tile.turned
            cols = slice(c * P, (c + 1) * P)
            src = ps.buf[:, :].rearrange("p (t c) -> p t c", t=KT)
            l = do("vector", lambda e: e.tensor_tensor(
                xn_lo[:, :, cols], src, xn_hi[:, :, cols].bitcast(F32), ALU.subtract), [h] + xn_read[c], k["lo"])
            ps.free = [l]
            xn_ready[c] = [h], [l]

        def rooms(b, j):
            if j == 0:
                return [(s, s.buf[:, at:at + BLK]) for s in decay.slots[1:] for at in (0, BLK)]
            if b == 0:
                return [(s, s.buf) for s in early_x[CPB:]]
            return [(s, s.buf[:, 0:BLK]) for s in (io, next_x)] + [
                (Slot(None), prefix_dt.buf[:, CPB:, :].rearrange("p c i -> p (c i)")),
                (yn.slots[1], yn.slots[1].buf[:, :])]

        def decay_rates():
            t = do("vector", lambda e: e.tensor_scalar(nega_sb[:, :], nega_sb[:, :], A_LOG_MAX, None, ALU.min),
                   [params], k["nega"])
            t = do("scalar", lambda e: e.activation(nega_sb[:, :], nega_sb[:, :], ACT.Exp), [t], k["nega"])
            nega_ready = do("vector", lambda e: e.tensor_scalar(nega_sb[:, :], nega_sb[:, :], -1.0, None, ALU.mult),
                            [t], k["nega"])
            return nega_ready

        def step_sizes(b, j):
            slots, (zs, es, us, ds) = zip(*rooms(b, j))
            free = [m for s in slots for m in s.free] + prefix_free[j]
            hi, lo = wout_hi, wout_lo
            cols = slice(j * BLK, (j + 1) * BLK)
            ps = big.take()
            mm = three_passes(ps.buf[:, :], [((hi[:, t, 0:P], lo[:, t, 0:P]), (xn_hi[:, t, cols],
                               xn_lo[:, t, cols])) for t in range(KT)],
                              w_ready["dt"], block_ready(j), ps.free, k["mm_dt"])
            z = do("scalar", lambda e, ps=ps, cols=cols: e.activation(
                zs, ps.buf[:, :], ACT.Identity, bias=dtb_sb[:, 0:1]), [mm, params] + free, k["z"])
            ps.free = [z]
            for c in range(j * CPB, (j + 1) * CPB):
                xn_read[c] = [mm]
            w_free["out"] = [mm]
            yield
            t = do("vector", lambda e: e.scalar_tensor_tensor(es, zs, -1.0, zs, ALU.mult, ALU.min),
                   [z] + free, k["absz"])
            t = do("scalar", lambda e: e.activation(es, es, ACT.Exp), [t], k["e"])
            yield
            u = do("vector", lambda e: e.tensor_scalar(us, es, 1.0, None, ALU.add), [t] + free, k["u"])
            t = do("vector", lambda e: e.scalar_tensor_tensor(es, us, -1.0, es, ALU.add, ALU.subtract),
                   [u], k["negc"])
            ln = do("scalar", lambda e: e.activation(ds, us, ACT.Ln), [u] + free, k["lnu"])
            ru = do("scalar", lambda e: e.activation(us, ds, ACT.Exp, scale=-1.0), [ln, t], k["ru"])
            yield
            if b == 1:
                yield
            t = do("vector", lambda e: e.tensor_tensor(es, es, us, ALU.mult), [ru], k["cru"])
            t = do("vector", lambda e: e.tensor_tensor(ds, ds, es, ALU.subtract), [t, ln], k["dt"])
            dt = do("vector", lambda e: e.scalar_tensor_tensor(ds, zs, 0.0, ds, ALU.max, ALU.add), [t], k["dt"])
            t = do("vector", lambda e: e.tensor_scalar(us, ds, nega_sb[:, 0:1], EXP_ZERO,
                                                       ALU.mult, ALU.max), [dt, rates_ready], k["da"])
            da = do("scalar", lambda e: e.activation(us, us, ACT.Exp), [t], k["da"])
            yield
            heads = slice(0, HEADS)
            starts = lambda buf: buf.rearrange("p (c i) -> p c i", i=P)[heads, :, 0:1]
            t1 = do("vector", lambda e: e.memset(zs, 0.0), [dt], k["dstart"])
            t0 = do("vector", lambda e: e.tensor_copy(es, us), [da], k["dz"])
            dz = do("vector", lambda e: e.memset(starts(es), 0.0), [t0], k["dz"])
            d1 = do("vector", lambda e: e.tensor_copy(starts(zs), starts(us)), [t1, da], k["dcopy"])
            pfx = do("vector", lambda e: e.tensor_tensor_scan(ds[heads, :], es[heads, :], zs[heads, :], 0.0,
                                                              ALU.mult, ALU.add), [dz, d1, da], k["pfx"])
            first = j * CPB
            std = do("sync", lambda e: e.dma_start(
                decays_d[b, first:first + CPB].rearrange("c h i -> h c i"),
                es[heads, :].rearrange("h (c i) -> h c i", i=P)), [dz], decays_marks[b][j], 16)
            yield
            ps = ps_u
            for i in range(CPB):
                mm = do("tensor", lambda e, i=i, ps=ps: e.transpose(
                    ps.buf[:, i * P:(i + 1) * P], ds[:, i * P:(i + 1) * P], eye),
                    [pfx] + ps.free, k["mm_pt"] if i == CPB - 1 else None)
            cp = do("scalar", lambda e, ps=ps: e.activation(
                prefix_dt.buf[:, first:first + CPB, :], ps.buf[:, :].rearrange("p (c i) -> p c i", i=P),
                ACT.Copy), [mm] + prefix_free[j], k["pt"])
            ps.free = [cp]
            stt = do("sync", lambda e: e.dma_start(totals_d[b:b + 1, first:first + CPB],
                                                   prefix_dt.buf[P - 1:P, first:first + CPB, 0:HEADS]),
                     [cp], totals_marks[b][j], 16)
            if b > 0:
                stp = do("sync", lambda e: e.dma_start(prefix_d[:, first:first + CPB, :],
                                                       prefix_dt.buf[:, first:first + CPB, :]), [cp],
                         prefix_stored[j], 16)
                prefix_free[j] = [stt, stp]
            else:
                loaded = do("sync", lambda e: e.dma_start(
                    total_bc.buf[:, first * HEADS:(first + CPB) * HEADS],
                    totals_d[b, first:first + CPB].rearrange("c h -> (c h)").partition_broadcast(P)),
                    [stt], totals_loaded[j], 16)
                prefix_ready[0][first:first + CPB] = [[cp, loaded]] * CPB
            for s in slots:
                s.free = [mm, std, d1]
            decays_stored[b][j] = [std]

        decays_stored = [[None] * NBLK for _ in range(BATCH)]
        prefix_ready = [[None] * NCH for _ in range(BATCH)]
        prefix_free = [[] for _ in range(NBLK)]
        decays_marks = [[mark(f"st_decays{b}{j}") for j in range(NBLK)] for b in range(BATCH)]
        totals_marks = [[mark(f"st_totals{b}{j}") for j in range(NBLK)] for b in range(BATCH)]
        prefix_stored = [mark(f"st_prefix{j}") for j in range(NBLK)]
        totals_loaded = [mark(f"landed_totals{j}") for j in range(NBLK)]

        def block_ready(j):
            return tuple([m for c in range(j * CPB, (j + 1) * CPB) for m in xn_ready[c][part]] for part in (0, 1))

        def reload_prefix(c):
            m = prefix_marks[c]
            hs = slice(c * HEADS, (c + 1) * HEADS)
            used = [(k[n], k[n].n) for n in ("cs", "dtx", "sdec")]
            do("sync", lambda e: e.dma_start(prefix_dt.buf[:, c, :], prefix_d[:, c, :]),
               used + [(prefix_stored[c // CPB], 16)], m, 16)
            t = do("sync", lambda e: e.dma_start(total_bc.buf[:, hs], totals_d[1, c].partition_broadcast(P)),
                   used + [(totals_marks[1][c // CPB], 16)], m, 16)
            prefix_ready[1][c] = [t]

        scratch = xc.slots[1].buf[:, :, :].rearrange("p m c -> p (m c)")
        lora_a_sb, lora_b_sb, lora_bs_sb, bias_sb = (scratch[:, i * DM:(i + 1) * DM] for i in range(4))

        room = xc.slots[0].buf[:, :, :].rearrange("p m c -> p (m c)")
        ffn_room = Slot(room[:, 0:KT * DM], mark("landed_ffn"))
        dt_room = Slot(room[:, KT * DM:KT * (DM + P)], mark("landed_dt"))

        def ffn_weights_fetch():
            for dst, src in ((lora_a_sb, lora_a), (lora_b_sb, lora_b_t), (bias_sb, ffn_bias.partition_broadcast(P))):
                got = do("sync", lambda e, dst=dst, src=src: e.dma_start(dst, src), (), k["wffn"], 16)
            raw = ffn_room.buf.rearrange("p (t c) -> p t c", t=KT)
            landed = do("sync", lambda e: e.dma_start(raw, w_ffn_t.rearrange("(t p) c -> p t c", p=P)),
                        (), ffn_room.mark, 16)
            return got, raw, landed

        def ffn_merge(got, raw, landed):
            loraw_ready = do("vector", lambda e: e.tensor_scalar(loraw_sb[:, :], loraw_sb[:, :], LORA_SCALE, None,
                                                                 ALU.mult), [lora_param], k["loraw"])
            scaled = do("vector", lambda e: e.tensor_scalar(lora_bs_sb, lora_b_sb, loraw_sb[:, 0:1], None,
                                                            ALU.mult), [got, loraw_ready], k["loraB"])
            for t in range(KT):
                ps = big.take()
                mm = do("tensor", lambda e, t=t, ps=ps: e.matmul(
                    ps.buf[:, :], lora_a_sb[:, t * P:(t + 1) * P], lora_bs_sb, start=True, stop=True),
                    [scaled, got] + ps.free, k["mm_ffn"])
                w = do("vector", lambda e, t=t, ps=ps: e.tensor_tensor(
                    raw[:, t, :], raw[:, t, :], ps.buf[:, :], ALU.add), [mm, landed], k["ffn_wl"])
                ps.free = [w]
                h = do("scalar", lambda e, t=t: e.activation(wgate_hi[:, t, :], raw[:, t, :], ACT.Copy),
                       [w], k["ffn_wh"])
                l = do("gpsimd", lambda e, t=t: e.tensor_tensor(
                    wgate_lo[:, t, :], raw[:, t, :], wgate_hi[:, t, :].bitcast(F32), ALU.subtract),
                    [w, h], k["ffn_lo"])
            xc.slots[0].free = [h, l]
            w_ready["ffn"] = [h], [l]

        ffn_out = Ring([sgate, x_tok])
        ffn_banks = Ring([ps_in, ps_cs])
        ffn_stored = [mark("ffn_stored0"), mark("ffn_stored1")]

        def ffn_chunk(b, c):
            cols = slice(c * P, (c + 1) * P)
            ps = ffn_banks.take()
            mm = three_passes(ps.buf[:, :], [((xn_hi[:, t, cols], xn_lo[:, t, cols]), (wgate_hi[:, t, :],
                               wgate_lo[:, t, :])) for t in range(KT)],
                              xn_ready[c], w_ready["ffn"], ps.free, k["mm_ffn"])
            xn_read[c] = [mm]
            w_free["gate"] = [mm]
            return ps, mm

        def ffn_finish(b, c, ps, mm):
            bd = do("vector", lambda e: e.tensor_tensor(y.buf[:, :], ps.buf[:, :], bias_sb, ALU.add),
                    [mm] + y.free, k["biased"])
            ps.free = [bd]
            o = ffn_out.take()
            a = do("scalar", lambda e: e.activation(o.buf[:, :], y.buf[:, :], ACT.Silu), [bd] + o.free, k["ffn_act"])
            y.free = [a]
            o.free = [do("sync", lambda e: e.dma_start(ffn_d[b, c], o.buf[:, :]), [a], ffn_stored[c % 2], 16)]
            xc.slots[1].free = [bd]

        tail_ready = [None] * MT
        pending_taps, pending_silus = [], []

        def finish_silus():
            while pending_silus:
                pending_silus.pop(0)()

        def finish_taps(keep=0):
            while len(pending_taps) > keep:
                pending_taps.pop(0)()

        def conv_tile(g, blk, m, slot, ready):
            tile = g * XT + m if m < XT else INNER // P + (m - XT) * GROUPS + g
            cols = slice(blk * BLK, (blk + 1) * BLK)
            mc = slice(m * P, (m + 1) * P)
            ps = big.take()
            mm = three_passes(ps.buf[:, :], [((wconv_hi[:, t, mc], wconv_lo[:, t, mc]), (xn_hi[:, t, cols],
                               xn_lo[:, t, cols])) for t in range(KT)],
                              w_ready["conv_x" if m < XT else "conv_bc"], block_ready(blk), ps.free, k["mm_conv"])
            h = halo.take()
            hb, acc = h.buf, slot.buf[:, m, :]
            full = do("scalar", lambda e: e.activation(hb[:, TAPS - 1:], ps.buf[:, :], ACT.Copy),
                      [mm] + h.free, k["h_full"])
            t0 = do("scalar", lambda e: e.activation(
                acc, ps.buf[:, :], ACT.Identity, bias=convb_sb[:, tile:tile + 1],
                scale=convw_sb[:, tile, TAPS - 1:TAPS]), [params] + slot.free, k["tap0"])
            ps.free = [t0, full]
            if blk == 0:
                head = do("gpsimd", lambda e: e.memset(hb[:, 0:TAPS - 1], 0.0), h.free, k["h_head"])
            else:
                head = do("gpsimd", lambda e: e.tensor_copy(hb[:, 0:TAPS - 1], tails[:, m, :]),
                          h.free + [tail_ready[m]], k["h_head"])
            h.free = []
            if blk < NBLK - 1:
                tail_ready[m] = do("gpsimd", lambda e: e.tensor_copy(tails[:, m, :], hb[:, BLK:]),
                                   [full, head], k["h_tail"])
                h.free = [tail_ready[m]]

            def taps():
                tok = t0
                for i in range(TAPS - 1):
                    tok = do("vector", lambda e, i=i: e.scalar_tensor_tensor(
                        acc, hb[:, i:i + BLK], convw_sb[:, tile, i:i + 1], acc, ALU.mult, ALU.add),
                        [tok, full, head], k["taps"])
                h.free = h.free + [tok]

                def silu():
                    ready[m] = do("scalar", lambda e: e.activation(acc, acc, ACT.Silu), [tok], k["silu"])

                pending_silus.append(silu)

            pending_taps.append(taps)
            return mm

        def heads_bc(ap, n=HD):
            return ap.unsqueeze(2).to_broadcast([P, GH, n])

        def by_head(ap):
            return ap.rearrange("p (h c) -> p h c", h=GH)

        def fetch_decays(ch):
            b, g, c = ch["b"], ch["g"], ch["c"]
            d = ch["decay"] = decay.take()
            src = decays_d[b, c, g * GH:(g + 1) * GH, :].rearrange("h i -> (h i)").partition_broadcast(P)
            ch["landed"] = do("sync", lambda e: e.dma_start(d.buf[:, :], src),
                              d.free + decays_stored[b][c // CPB], d.mark, 16)

        def load_stage(ch):
            g, c, slot, ready = ch["g"], ch["c"], ch["slot"], ch["ready"]
            cc = slice((c % CPB) * P, (c % CPB + 1) * P)
            ps = turned.take()
            for m in range(XT):
                tr = do("tensor", lambda e, m=m: e.transpose(
                    ps.buf[:, m * P:(m + 1) * P], slot.buf[:, m, cc], eye),
                    [ready[m], eye_ready] + ps.free, k["mm_t"] if m == XT - 1 else None)
            xt = do("scalar", lambda e: e.activation(x_tok.buf[:, :], ps.buf[:, :], ACT.Copy),
                    [tr] + x_tok.free, k["xt"])
            ps.free = [xt]
            dt_cols = prefix_dt.buf[:, c, HEADS + g * GH:HEADS + (g + 1) * GH]
            dx = ch["dtx"] = dtx.take()
            ch["dtx_t"] = do("vector", lambda e: e.tensor_tensor(
                by_head(dx.buf[:, :]), by_head(x_tok.buf[:, :]), heads_bc(dt_cols), ALU.mult),
                [xt] + prefix_ready[ch["b"]][c] + dx.free, k["dtx"])
            ch["xt"] = xt
            d = ch["decay"]
            sc = do("vector", lambda e: e.tensor_tensor_scan(
                d.buf[:, :], d.buf[:, :], eye8[:, :, :].rearrange("p h i -> p (h i)"), 0.0,
                ALU.mult, ALU.add), [ch["landed"], eye_ready], k["scan"])
            if c < NCH - 1:
                w = xw
                ch["xw_t"] = do("vector", lambda e: e.tensor_tensor(
                    by_head(w.buf[:, :]), by_head(dx.buf[:, :]),
                    by_head(d.buf[:, :])[:, :, P - 1:P].to_broadcast([P, GH, HD]), ALU.mult),
                    [ch["dtx_t"], sc] + w.free, k["xw"])
            ch["scan"] = sc

        def mask_stage(ch):
            c, slot, ready = ch["c"], ch["slot"], ch["ready"]
            cc = slice((c % CPB) * P, (c % CPB + 1) * P)
            if c < NCH - 1:
                bt = do("tensor", lambda e: e.transpose(ps_u.buf[:, 0:P], slot.buf[:, XT, cc], eye),
                        [ready[XT]] + ps_u.free, k["mm_bt"])
                hi, lo = ch["b_hi"], ch["b_lo"] = b_hi.take(), b_lo.take()
                h = do("scalar", lambda e: e.activation(hi.buf[:, :], ps_u.buf[:, 0:P], ACT.Copy),
                       [bt] + hi.free, k["bt"])
                l = do("vector", lambda e: e.tensor_tensor(
                    lo.buf[:, :], ps_u.buf[:, 0:P], hi.buf[:, :].bitcast(F32), ALU.subtract),
                    [h] + lo.free, k["bt_lo"])
                ch["bt"] = [h], [l]
                ps_u.free = [l]
            gm = do("tensor", lambda e: e.matmul(ps_g.buf[:, 0:P], slot.buf[:, XT, cc], slot.buf[:, XT + 1, cc],
                                                 start=True, stop=True),
                    [ready[XT], ready[XT + 1]] + ps_g.free, k["mm_g"])
            ch["gm"] = gm

        def product_stage(ch):
            d = ch["decay"]
            ch["M_t"] = do("vector", lambda e: e.tensor_tensor(
                by_head(d.buf[:, :]), by_head(d.buf[:, :]),
                ps_g.buf[:, 0:P].unsqueeze(1).to_broadcast([P, GH, P]), ALU.mult),
                [ch["scan"], ch["gm"]] + ([ch["xw_t"]] if ch["c"] < NCH - 1 else []), k["M"])
            ps_g.free = [ch["M_t"]]

        def weighted_stage(ch):
            if ch["c"] == NCH - 1:
                return
            h = do("scalar", lambda e: e.activation(xw_hi.buf[:, :], xw.buf[:, :], ACT.Copy),
                   [ch["xw_t"]] + xw_hi.free, k["xw_hi"])
            l = do("gpsimd", lambda e: e.tensor_tensor(
                xw_lo.buf[:, :], xw.buf[:, :], xw_hi.buf[:, :].bitcast(F32), ALU.subtract),
                [ch["xw_t"], h] + xw_lo.free, k["xw_lo"])
            xw.free = [h, l]
            ch["xw_parts"] = [h], [l]

        def skip_stage(ch):
            g = ch["g"]
            ch["skip_t"] = do("gpsimd", lambda e: e.tensor_tensor(
                by_head(skip.buf[:, :]), by_head(x_tok.buf[:, :]),
                heads_bc(skip_bc[:, g * GH:(g + 1) * GH]), ALU.mult), [ch["xt"], params] + skip.free, k["skip"])
            x_tok.free = [ch["dtx_t"], ch["skip_t"]]

        def gate_project(ch):
            c = ch["c"]
            cols = slice(c * P, (c + 1) * P)
            ps = big.take()
            mm = three_passes(ps.buf[:, :], [((xn_hi[:, t, cols], xn_lo[:, t, cols]), (wgate_hi[:, t, :],
                               wgate_lo[:, t, :])) for t in range(KT)],
                              xn_ready[c], w_ready["gate"], ps.free, k["mm_gate"])
            w_free["gate"] = [mm]
            xn_read[c] = [mm, last_conv[c // CPB]]
            ch["gate"] = ps, mm

        def gate_silu(ch):
            ps, mm = ch["gate"]
            ch["sgate_t"] = do("scalar", lambda e: e.activation(sgate.buf[:, :], ps.buf[:, :], ACT.Silu),
                               [mm] + sgate.free, k["sgate"])
            ps.free = [ch["sgate_t"]]

        def mix_stage(ch):
            g, c, slot = ch["g"], ch["c"], ch["slot"]
            cc = slice((c % CPB) * P, (c % CPB + 1) * P)
            dx, mx = ch["dtx"], ch["decay"]
            tok = None
            if c > 0:
                s = ch["state_in"]
                tok = do("tensor", lambda e: e.matmul(ps_cs.buf[:, :], slot.buf[:, XT + 1, cc], s.buf[:, :],
                                                      start=True, stop=True),
                         [ch["state_t"]] + ps_cs.free, k["mm_cs"])
            for h in range(GH):
                n = 2 * HD if h < GH - 1 else HD
                mi = do("tensor", lambda e, h=h, n=n: e.matmul(
                    ps_in.buf[:, h * HD:h * HD + n], mx.buf[:, h * P:(h + 1) * P],
                    dx.buf[:, h * HD:h * HD + n], start=True, stop=True, skip_group_check=True),
                    [ch["M_t"], ch["dtx_t"]] + ps_in.free, k["mm_in"] if h == GH - 1 else None)
            dx.free, mx.free = [mi], [mi]
            if c < NCH - 1:
                hi, lo = ch["b_hi"], ch["b_lo"]
                mu = three_passes(ps_u.buf[:, :], [((hi.buf[:, :], lo.buf[:, :]), (xw_hi.buf[:, :], xw_lo.buf[:, :]))],
                                  ch["bt"], ch["xw_parts"], ps_u.free, k["mm_u"], a_lo_last=True)
                xw_hi.free = xw_lo.free = hi.free = lo.free = [mu]
            ch["last_pe"] = mi
            if c > 0:
                cs = do("vector", lambda e: e.tensor_tensor(
                    by_head(y.buf[:, :]), by_head(ps_cs.buf[:, :]),
                    heads_bc(prefix_dt.buf[:, c, g * GH:(g + 1) * GH]), ALU.mult),
                    [tok] + prefix_ready[ch["b"]][c] + y.free, k["cs"])
                ps_cs.free = [cs]
                y1 = do("vector", lambda e: e.tensor_tensor(y.buf[:, :], ps_in.buf[:, :], y.buf[:, :], ALU.add),
                        [mi, cs], k["y1"])
                ps_in.free = [y1]
            if c < NCH - 1:
                if c > 0:
                    new = ch["state_out"]
                    st = do("vector", lambda e: e.tensor_tensor(
                        new.buf[:, :], ps_u.buf[:, :], new.buf[:, :], ALU.add), [mu, ch["sdec_t"]], k["state"])
                else:
                    new = state.take()
                    st = do("vector", lambda e: e.tensor_copy(new.buf[:, :], ps_u.buf[:, :]),
                            [mu] + new.free, k["state"])
                ps_u.free = [st]
                ch["next"]["state_in"], ch["next"]["state_t"] = new, st
            if c > 0:
                y2 = do("vector", lambda e: e.tensor_tensor(y.buf[:, :], y.buf[:, :], skip.buf[:, :], ALU.add),
                        [y1, ch["skip_t"]], k["y2"])
            else:
                y2 = do("vector", lambda e: e.tensor_tensor(y.buf[:, :], ps_in.buf[:, :], skip.buf[:, :], ALU.add),
                        [mi, ch["skip_t"]] + y.free, k["y2"])
                ps_in.free = [y2]
            skip.free = [y2]
            ch["y2"] = y2
            if c > 0:
                ch["state_in"].free = ch["state_in"].free + [tok]
            if 0 < c + 1 < NCH - 1:
                tot = total_bc.buf[:, (c + 1) * HEADS + g * GH:(c + 1) * HEADS + (g + 1) * GH]
                dec = ch["next"]["state_out"] = state.take()
                ch["next"]["sdec_t"] = do("gpsimd", lambda e: e.tensor_tensor(
                    by_head(dec.buf[:, :]), by_head(new.buf[:, :]), heads_bc(tot), ALU.mult),
                    [st] + prefix_ready[ch["b"]][c + 1] + dec.free, k["sdec"])
                new.free = [ch["next"]["sdec_t"]]
            elif c < NCH - 1:
                new.free = []

        def norm_stage(ch):
            n_ = ch["yn"] = yn.take()
            sq = do("scalar", lambda e: e.activation(n_.buf[:, :], y.buf[:, :], ACT.Square,
                                                     accum_out=square_sum[:, :]),
                    [ch["y2"]] + n_.free + [(k["rstd2"], k["rstd2"].n)], k["ssq"])
            v = do("gpsimd", lambda e: e.tensor_scalar(
                mean_square[:, :], square_sum[:, :], 1.0 / GC, EPS, ALU.mult, ALU.add), [sq], k["var2"])
            ch["rstd_t"] = do("gpsimd", lambda e: e.tensor_tensor(
                rstd_col[:, :], mean_square[:, :], half[:, :], ALU.pow),
                              [v, half_ready, (k["yn"], k["yn"].n)], k["rstd2"])

        def gated_stage(ch):
            ch["yn_t"] = do("vector", lambda e: e.scalar_tensor_tensor(
                ch["yn"].buf[:, :], y.buf[:, :], rstd_col[:, 0:1], sgate.buf[:, :], ALU.mult, ALU.mult),
                [ch["rstd_t"], ch["sgate_t"]], k["yn"])
            y.free = [ch["yn_t"]]
            sgate.free = [ch["yn_t"]]

        def turn_stage(ch):
            ps = turned.take()
            for t in range(XT):
                tr = do("tensor", lambda e, t=t: e.transpose(
                    ps.buf[:, t * P:(t + 1) * P], ch["yn"].buf[:, t * P:(t + 1) * P], eye),
                    [ch["yn_t"]] + ps.free, k["mm_ynt"] if t == XT - 1 else None)
            ch["yn"].free = [tr]
            src = ps.buf[:, :].rearrange("p (t c) -> p t c", t=XT)
            h = do("scalar", lambda e: e.activation(ynt_hi.buf[:, :, :], src, ACT.Copy),
                   [tr] + ynt_hi.free, k["hi2"])
            ch["turned"] = ps, src, h

        def turn_split(ch):
            ps, src, h = ch["turned"]
            l = do("vector", lambda e: e.tensor_tensor(ynt_lo.buf[:, :, :], src, ynt_hi.buf[:, :, :].bitcast(F32),
                                                       ALU.subtract), [h] + ynt_lo.free, k["lo2"])
            ps.free = [l]
            ch["ynt"] = [h], [l]

        def project_stage(ch):
            b, g, c = ch["b"], ch["g"], ch["c"]
            ps = big.take()
            mm = three_passes(ps.buf[:, :], [((ynt_hi.buf[:, t, :], ynt_lo.buf[:, t, :]), (wout_hi[:, t, :],
                               wout_lo[:, t, :])) for t in range(XT)],
                              ch["ynt"], w_ready["out"], ps.free, k["mm_out"])
            ynt_hi.free = ynt_lo.free = [mm]
            w_free["out"] = [mm]
            ch["projected"] = ps, mm

        def sum_stage(ch):
            g, c = ch["g"], ch["c"]
            ps, mm = ch["projected"]
            acc = out_sum[:, c, :]
            if g == 0:
                o = do("vector", lambda e: e.tensor_copy(acc, ps.buf[:, :]), [mm] + stored[c], k["osum"])
            else:
                o = do("vector", lambda e: e.tensor_tensor(acc, acc, ps.buf[:, :], ALU.add),
                       [mm, sum_ready[c]], k["osum"])
            ps.free = [o]
            sum_ready[c] = o


        def final_fetch(ch):
            b, c = ch["b"], ch["c"]
            ch["linear"] = do("sync", lambda e: e.dma_start(io.buf[:, :], ffn_d[b, c]),
                              io.free + [(m, m.n) for m in ffn_stored], io.mark, 16)
            ch["x_room"] = next_x if b > 0 else io
            if b > 0:
                final_fetch_x(ch)

        def final_fetch_x(ch):
            b, c, room = ch["b"], ch["c"], ch["x_room"]
            ch["x"] = do("sync", lambda e: e.dma_start(room.buf[:, :], hidden[b, c * P:(c + 1) * P, :]),
                         room.free, room.mark, 16)

        def final_multiply(ch):
            acc = out_sum[:, ch["c"], :]
            ch["product"] = do("gpsimd", lambda e: e.tensor_tensor(acc, acc, io.buf[:, :], ALU.mult),
                               [sum_ready[ch["c"]], ch["linear"]], k["fin1"])
            io.free = [ch["product"]]
            if ch["b"] == 0:
                final_fetch_x(ch)

        def final_add(ch):
            b, c, room = ch["b"], ch["c"], ch["x_room"]
            acc = out_sum[:, c, :]
            f = do("gpsimd", lambda e: e.tensor_tensor(acc, acc, room.buf[:, :], ALU.add),
                   [ch["product"], ch["x"]], k["fin2"])
            room.free = [f]
            stored[c] = [do("sync", lambda e: e.dma_start(out[b, c * P:(c + 1) * P, :], acc), [f],
                            k["stored"], 16)]

        stored = [[] for _ in range(NCH)]
        sum_ready = [None] * NCH

        early_x = [Slot(out_sum[:, c, :], mark(f"landed_x{c}")) for c in range(NCH)]
        tokens = [(b, c) for b in (1, 0) for c in range(NCH)]
        norm_fetch(1, 0, early_x[0])
        norm_fetch(1, 1, early_x[1])
        ffn_raw = ffn_weights_fetch()
        fetch_weight("dt", 0, dt_room)
        for c in range(2, NCH):
            norm_fetch(1, c, early_x[c])
        fetch_weight("conv_x", 0)
        fetch_weight("conv_bc", 0)
        products, chains, held = {}, [], None
        lag = 4

        NG = GROUPS * NBLK * BATCH
        last_conv = [None] * NBLK
        blocks, chunks = [], []
        for i in range(NG):
            bl = dict(b=i // (GROUPS * NBLK), g=i // NBLK % GROUPS, blk=i % NBLK, slot=xc.slots[i % 2],
                      ready=[None] * MT)
            blocks.append(bl)
            chunks += [dict(bl, c=bl["blk"] * CPB + j, block=i) for j in range(CPB)]
        for a, nxt in zip(chunks, chunks[1:]):
            a["next"] = nxt
        n = len(chunks)
        early = [[[], [1], [3], [5]]] * NG
        late = [[[0], [2], [4], []]] * NG
        early[NG // 2], late[NG // 2] = [[], [0], [2], [4]], [[], [1], [3], [5]]

        def conv_tiles(nb, tiles):
            if nb == NG:
                return
            bl = blocks[nb]
            for m in tiles:
                mm = conv_tile(bl["g"], bl["blk"], m, bl["slot"], bl["ready"])
                last_conv[bl["blk"]] = mm
                w_free["conv_x" if m < XT else "conv_bc"] = [mm]
                finish_taps(1)

        def swap_weights(i):
            group, at = divmod(i, NCH)
            g, nxt = group % GROUPS, (group + 1) % GROUPS
            left = BATCH * GROUPS - 1 - group
            if at == 0:
                split_weight("gate")
                fetch_weight("out", g)
            if at == 1:
                scale_out_weight()
            if at == 2 and left:
                split_weight("conv_x")
                fetch_weight("conv_bc", nxt)
            if at == 3 and left:
                fetch_weight("gate", nxt)
            if at == 4 and left:
                split_weight("conv_bc")
                if left > 1:
                    fetch_weight("conv_x", (nxt + 1) % GROUPS)

        def advance(held=None):
            return [x for x in chains if x is held or next(x, 0) is None]

        for s in range(len(tokens) + lag):
            new, norm, split, multiply, finish = (
                tokens[s - back] if 0 <= s - back < len(tokens) else None for back in range(lag + 1))
            if new:
                norm_stats(new[1], early_x[new[1]])
            if norm:
                b, c = norm
                norm_apply(c, early_x[c])
                norm_turn(c, early_x[c])
                if b == 1:
                    norm_fetch(0, c, early_x[c])
            if s == 1:
                ffn_merge(*ffn_raw)
            if s == 3:
                split_weight("dt")
                rates_ready = decay_rates()
            if split:
                norm_split(split[1], early_x[split[1]])
            if multiply:
                products[multiply] = ffn_chunk(*multiply)
            if finish:
                ffn_finish(*finish, *products.pop(finish))
            if multiply and multiply[1] % CPB == CPB - 1:
                held = step_sizes(multiply[0], multiply[1] // CPB)
                chains.append(held)
            chains = advance(held if s == len(tokens) + lag - 1 else None)
            if 3 <= s < 3 + KT:
                split_weight("conv_x", [s - 3])
            if s == 3 + KT:
                fetch_weight("gate", 0)
            if 8 <= s < 8 + KT:
                split_weight("conv_bc", [s - 8])
            if s == 8 + KT:
                fetch_weight("conv_x", 1)
            if 14 <= s < 14 + MT:
                conv_tiles(0, [s - 14])
                finish_silus()
        finish_taps()
        finish_silus()

        fetch_decays(chunks[0])
        lo_engines = ("gpsimd", "vector", "gpsimd", "gpsimd")
        adding = None
        behind = n // 2 - NCH + 1
        for i in range(n + 4):
            chunk = chunks[i] if i < n else None
            mixed = chunks[i - 1] if 1 <= i < n + 1 else None
            turning = chunks[i - 3] if 3 <= i < n + 3 else None
            summed = chunks[i - 4] if i >= 4 else None
            last = summed if summed and summed["g"] == GROUPS - 1 else None
            moving = i - behind if 0 <= i - behind < NCH else None
            if i + 1 < n:
                fetch_decays(chunks[i + 1])
            if i + 1 == behind:
                norm_fetch(1, 0, next_x)
            if chunk:
                load_stage(chunk)
                if moving is not None:
                    norm_stats(moving, next_x)
                conv_tiles(chunk["block"] + 1, early[(chunk["block"] + 1) % NG][i % CPB])
                if i % 2 == 0:
                    chains = advance()
            if adding:
                final_add(adding)
                adding = None
            if last:
                final_fetch(last)
            if summed:
                project_stage(summed)
            if chunk and i % NCH == 3:
                split_weight("out", [0, 1], lo_engines)
            if turning:
                turn_stage(turning)
            if moving is not None:
                norm_apply(moving, next_x)
            if mixed:
                gate_project(mixed)
            if chunk:
                mask_stage(chunk)
                if i % NCH == 3:
                    split_weight("out", [2, 3], lo_engines)
            if summed:
                sum_stage(summed)
            if turning:
                turn_split(turning)
            if mixed:
                gate_silu(mixed)
            finish_silus()
            if chunk:
                swap_weights(i)
            if mixed:
                mix_stage(mixed)
                if moving is not None:
                    norm_turn(moving, next_x)
                    norm_split(moving, next_x)
                    if moving + 1 < NCH:
                        norm_fetch(1, moving + 1, next_x)
                    reload_prefix(moving)
                norm_stage(mixed)
                if mixed["c"] % CPB == CPB - 1:
                    mixed["slot"].free = [mixed["last_pe"]]
            if chunk:
                product_stage(chunk)
                skip_stage(chunk)
                weighted_stage(chunk)
                conv_tiles(chunk["block"] + 1, late[(chunk["block"] + 1) % NG][i % CPB])
                if i % CPB == CPB - 1:
                    finish_taps()
                finish_silus()
            if mixed:
                gated_stage(mixed)
            if last:
                final_multiply(last)
                if last["b"] > 0:
                    final_add(last)
                else:
                    adding = last
            chains = advance()
        stores = [k["stored"]] + sum(decays_marks + totals_marks, []) + prefix_stored + ffn_stored
        q.wait("sync", [(m, m.n) for m in stores])

        block = ctx.enter_context(nc.Block())

        @block.sync
        def _(e):
            q.play("sync", e)

        @block.scalar
        def _(e):
            q.play("scalar", e)

        @block.vector
        def _(e):
            q.play("vector", e)

        @block.gpsimd
        def _(e):
            q.play("gpsimd", e)

        @block.tensor
        def _(e):
            q.play("tensor", e)


def kernel(L0_attn_hidden_states, L0_attn_in_proj_w, L0_attn_conv_weight, L0_attn_conv_bias, L0_attn_dt_bias,
           L0_attn_A_log, L0_attn_D, L0_attn_norm_weight, L0_attn_out_proj_w, L0_ffn_lora_A, L0_ffn_lora_B,
           L0_ffn_W, L0_ffn_bias, L0_ffn_lora_weights):
    import numpy as np
    import concourse.bacc as bacc
    from concourse.bass_utils import run_bass_kernel_spmd

    lay = np.ascontiguousarray
    arrays = {
        "hidden": lay(L0_attn_hidden_states),
        "w_in_t": lay(np.asarray(L0_attn_in_proj_w).T),
        "conv_w": lay(np.asarray(L0_attn_conv_weight).reshape(CONV // P, P, TAPS).transpose(1, 0, 2)),
        "conv_b": lay(np.asarray(L0_attn_conv_bias).reshape(CONV // P, P).T),
        "dt_bias": lay(L0_attn_dt_bias).reshape(HEADS, 1),
        "a_log": lay(L0_attn_A_log).reshape(HEADS, 1),
        "d_skip": lay(L0_attn_D),
        "norm_w": lay(np.asarray(L0_attn_norm_weight).reshape(INNER // P, P).T),
        "w_out_t": lay(np.asarray(L0_attn_out_proj_w).T),
        "lora_a": lay(L0_ffn_lora_A).reshape(LORA_N * LORA_R, DM),
        "lora_b_t": lay(np.asarray(L0_ffn_lora_B).transpose(0, 2, 1)).reshape(LORA_N * LORA_R, DM),
        "w_ffn_t": lay(np.asarray(L0_ffn_W).T),
        "ffn_bias": lay(L0_ffn_bias),
        "lora_w": lay(np.repeat(np.asarray(L0_ffn_lora_weights), LORA_R)).reshape(LORA_N * LORA_R, 1),
    }
    nc = bacc.Bacc("TRN2", target_bir_lowering=False, num_devices=1)
    args = [nc.dram_tensor(name, a.shape, mybir.dt.from_np(a.dtype), kind="ExternalInput").ap()
            for name, a in arrays.items()]
    out = nc.dram_tensor("out", (BATCH, SEQ, DM), F32, kind="ExternalOutput").ap()
    build(nc, *args, out)
    r = run_bass_kernel_spmd(nc, [arrays], core_ids=[0])
    return r.results[0]["out"]
```
